# Optimizing a Trainium2 kernel written in Bass

```python
import numpy as np
import jax
import jax.numpy as jnp

def _softmax(x, axis=-1):
    return jax.nn.softmax(x, axis=axis)

def _gelu(x):
    return jax.nn.gelu(x, approximate=True)

def _silu(x):
    return jax.nn.silu(x)

def _sigmoid(x):
    return jax.nn.sigmoid(x)

def _layernorm(x, axis=-1, eps=1e-05):
    m = jnp.mean(x, axis=axis, keepdims=True)
    v = jnp.var(x, axis=axis, keepdims=True)
    return (x - m) / jnp.sqrt(v + eps)

def _scatter_add(tgt, idx, src, axis=0):
    return tgt.at[idx].add(src)

def _segment_sum(src, seg, n):
    return jax.ops.segment_sum(src, seg, n)
kernel_name = 'mk_gnn_ffn_d1_gnn_r8_a1a64c'

def setup_inputs(seed: int=0):
    np.random.seed(seed)
    _w = jnp.asarray

    def _rec_inputs():
        import jax
        import jax.numpy as jnp
        _gk = jax.random.key(seed)
        x = -0.0003713 + 1 * jax.random.normal(jax.random.fold_in(_gk, 1), (12500, 256), jnp.float32)
        _s = jax.random.randint(jax.random.fold_in(_gk, 2), (100000,), 0, 12500, jnp.int32)
        _d = jax.random.randint(jax.random.fold_in(_gk, 3), (100000,), 0, 12500, jnp.int32)
        _loop = jnp.arange(12500, dtype=jnp.int32)
        src = jnp.concatenate([_s, _d, _loop])
        dst = jnp.concatenate([_d, _s, _loop])
        _o = jnp.argsort(dst, stable=True)
        src = src[_o]
        dst = dst[_o]
        edge_attr_32 = 0.000189758 + 1.00013 * jax.random.normal(jax.random.fold_in(_gk, 11), (212500, 32), jnp.float32)
        return (x, src, dst, edge_attr_32)
    x, src, dst, edge_attr_32 = _rec_inputs()

    def _L0_gnn_setup():
        import jax, jax.numpy as jnp
        import numpy as np
        N_NODES = 6250
        N_EDGES = 200000
        IN_CH = 256
        ADAPTER = 64
        EDGE_DIM = 32
        key = jax.random.key(seed)
        ks = jax.random.split(key, 12)
        s = lambda k, shape: jax.random.normal(k, shape, dtype=jnp.float32) * 0.05
        x = jax.random.normal(ks[0], (N_NODES, IN_CH), dtype=jnp.float32)
        edge_index = jax.random.randint(ks[1], (2, N_EDGES), 0, N_NODES, dtype=jnp.int64)
        edge_attr = jax.random.normal(ks[2], (N_EDGES, EDGE_DIM), dtype=jnp.float32)
        return {'x': x, 'edge_index': edge_index, 'edge_attr': edge_attr, 'W_down': s(ks[3], (ADAPTER, IN_CH)), 'b_down': jnp.zeros((ADAPTER,), jnp.float32), 'W_time': s(ks[4], (ADAPTER, EDGE_DIM)), 'b_time': jnp.zeros((ADAPTER,), jnp.float32), 'W_fusion': s(ks[5], (ADAPTER, 2 * ADAPTER)), 'b_fusion': jnp.zeros((ADAPTER,), jnp.float32), 'W_up': s(ks[6], (IN_CH, ADAPTER)), 'b_up': jnp.zeros((IN_CH,), jnp.float32)}
    _L0_gnn_all = _L0_gnn_setup()
    _L0_gnn_in = {k: v for k, v in _L0_gnn_all.items() if k in ('W_down', 'b_down', 'W_time', 'b_time', 'W_fusion', 'b_fusion', 'W_up', 'b_up')}
    del _L0_gnn_all

    def _L0_ffn_setup():
        import jax, jax.numpy as jnp
        import numpy as np
        B, A = (512, 8)
        IN, OUT = (256, 256)
        SH1, SH2 = (256, 128)
        EH1, EH2 = (128, 64)
        E, TOPK = (4, 2)

        def _shared_mlp(x, W1, b1, W2, b2, W3, b3):
            h = jax.nn.relu(x @ W1 + b1)
            h = jax.nn.relu(h @ W2 + b2)
            return h @ W3 + b3

        def _experts_mlp(x, eW1, eb1, eW2, eb2, eW3, eb3):
            h = jax.nn.relu(jnp.einsum('baf,efh->ebah', x, eW1) + eb1[:, None, None, :])
            h = jax.nn.relu(jnp.einsum('ebah,ehg->ebag', h, eW2) + eb2[:, None, None, :])
            o = jnp.einsum('ebag,ego->ebao', h, eW3) + eb3[:, None, None, :]
            return jnp.moveaxis(o, 0, -1)
        key = jax.random.key(seed)
        ks = jax.random.split(key, 16)
        s = 0.05
        return {'x': jax.random.normal(ks[0], (B, A, IN), jnp.float32), 'sW1': jax.random.normal(ks[1], (IN, SH1), jnp.float32) * s, 'sb1': jnp.zeros((SH1,), jnp.float32), 'sW2': jax.random.normal(ks[2], (SH1, SH2), jnp.float32) * s, 'sb2': jnp.zeros((SH2,), jnp.float32), 'sW3': jax.random.normal(ks[3], (SH2, OUT), jnp.float32) * s, 'sb3': jnp.zeros((OUT,), jnp.float32), 'eW1': jax.random.normal(ks[4], (E, IN, EH1), jnp.float32) * s, 'eb1': jnp.zeros((E, EH1), jnp.float32), 'eW2': jax.random.normal(ks[5], (E, EH1, EH2), jnp.float32) * s, 'eb2': jnp.zeros((E, EH2), jnp.float32), 'eW3': jax.random.normal(ks[6], (E, EH2, OUT), jnp.float32) * s, 'eb3': jnp.zeros((E, OUT), jnp.float32), 'gW': jax.random.normal(ks[7], (IN, E), jnp.float32) * s, 'gb': jnp.zeros((E,), jnp.float32)}
    _L0_ffn_all = _L0_ffn_setup()
    _L0_ffn_in = {k: v for k, v in _L0_ffn_all.items() if k in ('sW1', 'sb1', 'sW2', 'sb2', 'sW3', 'sb3', 'eW1', 'eb1', 'eW2', 'eb2', 'eW3', 'eb3', 'gW', 'gb')}
    del _L0_ffn_all
    return {'x': x, 'src': src, 'dst': dst, 'edge_attr_32': edge_attr_32, 'L0_gnn_W_down': _L0_gnn_in['W_down'], 'L0_gnn_b_down': _L0_gnn_in['b_down'], 'L0_gnn_W_time': _L0_gnn_in['W_time'], 'L0_gnn_b_time': _L0_gnn_in['b_time'], 'L0_gnn_W_fusion': _L0_gnn_in['W_fusion'], 'L0_gnn_b_fusion': _L0_gnn_in['b_fusion'], 'L0_gnn_W_up': _L0_gnn_in['W_up'], 'L0_gnn_b_up': _L0_gnn_in['b_up'], 'L0_ffn_sW1': _L0_ffn_in['sW1'], 'L0_ffn_sb1': _L0_ffn_in['sb1'], 'L0_ffn_sW2': _L0_ffn_in['sW2'], 'L0_ffn_sb2': _L0_ffn_in['sb2'], 'L0_ffn_sW3': _L0_ffn_in['sW3'], 'L0_ffn_sb3': _L0_ffn_in['sb3'], 'L0_ffn_eW1': _L0_ffn_in['eW1'], 'L0_ffn_eb1': _L0_ffn_in['eb1'], 'L0_ffn_eW2': _L0_ffn_in['eW2'], 'L0_ffn_eb2': _L0_ffn_in['eb2'], 'L0_ffn_eW3': _L0_ffn_in['eW3'], 'L0_ffn_eb3': _L0_ffn_in['eb3'], 'L0_ffn_gW': _L0_ffn_in['gW'], 'L0_ffn_gb': _L0_ffn_in['gb']}

def reference(x, src, dst, edge_attr_32, L0_gnn_W_down, L0_gnn_b_down, L0_gnn_W_time, L0_gnn_b_time, L0_gnn_W_fusion, L0_gnn_b_fusion, L0_gnn_W_up, L0_gnn_b_up, L0_ffn_sW1, L0_ffn_sb1, L0_ffn_sW2, L0_ffn_sb2, L0_ffn_sW3, L0_ffn_sb3, L0_ffn_eW1, L0_ffn_eb1, L0_ffn_eW2, L0_ffn_eb2, L0_ffn_eW3, L0_ffn_eb3, L0_ffn_gW, L0_ffn_gb):
    import jax
    import jax.numpy as jnp

    def _L0_gnn_ref(x, edge_index, edge_attr, W_down, b_down, W_time, b_time, W_fusion, b_fusion, W_up, b_up):
        import jax, jax.numpy as jnp
        import numpy as np
        N_NODES = 6250
        N_EDGES = 200000
        IN_CH = 256
        ADAPTER = 64
        EDGE_DIM = 32
        n = x.shape[0]
        node_feat = jax.nn.relu(x @ W_down.T + b_down)
        time_feat = jax.nn.relu(edge_attr @ W_time.T + b_time)
        src = edge_index[0]
        sums = jax.ops.segment_sum(time_feat, src, num_segments=n)
        counts = jax.ops.segment_sum(jnp.ones((time_feat.shape[0],), jnp.float32), src, num_segments=n)
        node_time_feat = sums / jnp.maximum(counts, 1.0)[:, None]
        combined = jnp.concatenate([node_feat, node_time_feat], axis=-1)
        fused = jax.nn.relu(combined @ W_fusion.T + b_fusion)
        out = fused @ W_up.T + b_up
        return x + out

    def _L0_ffn_ref(x, sW1, sb1, sW2, sb2, sW3, sb3, eW1, eb1, eW2, eb2, eW3, eb3, gW, gb):
        import jax, jax.numpy as jnp
        import numpy as np
        B, A = (512, 8)
        IN, OUT = (256, 256)
        SH1, SH2 = (256, 128)
        EH1, EH2 = (128, 64)
        E, TOPK = (4, 2)

        def _shared_mlp(x, W1, b1, W2, b2, W3, b3):
            h = jax.nn.relu(x @ W1 + b1)
            h = jax.nn.relu(h @ W2 + b2)
            return h @ W3 + b3

        def _experts_mlp(x, eW1, eb1, eW2, eb2, eW3, eb3):
            h = jax.nn.relu(jnp.einsum('baf,efh->ebah', x, eW1) + eb1[:, None, None, :])
            h = jax.nn.relu(jnp.einsum('ebah,ehg->ebag', h, eW2) + eb2[:, None, None, :])
            o = jnp.einsum('ebag,ego->ebao', h, eW3) + eb3[:, None, None, :]
            return jnp.moveaxis(o, 0, -1)
        all_out = _experts_mlp(x, eW1, eb1, eW2, eb2, eW3, eb3)
        shared = _shared_mlp(x, sW1, sb1, sW2, sb2, sW3, sb3)
        gates = jax.nn.softmax(x @ gW + gb, axis=-1)
        topv, topi = jax.lax.top_k(gates, TOPK)
        topw = jax.nn.softmax(topv, axis=-1)
        sel = jnp.take_along_axis(all_out, topi[:, :, None, :], axis=-1)
        gated = jnp.sum(sel * topw[:, :, None, :], axis=-1)
        return shared + gated
    edge_index = jnp.stack([src, dst])
    x = x + _L0_gnn_ref(_layernorm(x, axis=-1), edge_index, edge_attr_32, L0_gnn_W_down, L0_gnn_b_down, L0_gnn_W_time, L0_gnn_b_time, L0_gnn_W_fusion, L0_gnn_b_fusion, L0_gnn_W_up, L0_gnn_b_up)
    x = x + _L0_ffn_ref(_layernorm(x, axis=-1)[None], L0_ffn_sW1, L0_ffn_sb1, L0_ffn_sW2, L0_ffn_sb2, L0_ffn_sW3, L0_ffn_sb3, L0_ffn_eW1, L0_ffn_eb1, L0_ffn_eW2, L0_ffn_eb2, L0_ffn_eW3, L0_ffn_eb3, L0_ffn_gW, L0_ffn_gb)[0]
    return x

_drawn_inputs = setup_inputs


def setup_inputs(seed=0):
    import zlib

    import numpy as np

    out = dict(_drawn_inputs(seed))
    spreads = {'L0_gnn_b_down': (0.0, 2.0),
     'L0_gnn_b_time': (0.0, 2.0),
     'L0_gnn_b_fusion': (0.0, 0.46),
     'L0_gnn_b_up': (0.0, 0.1),
     'L0_ffn_sb1': (0.0, 0.789),
     'L0_ffn_sb2': (0.0, 0.377),
     'L0_ffn_sb3': (0.0, 0.1),
     'L0_ffn_eb1': (0.0, 2.0),
     'L0_ffn_eb2': (0.0, 0.8),
     'L0_ffn_eb3': (0.0, 0.1),
     'L0_ffn_gb': (0.0, 0.708)}
    factors = {'edge_attr_32': 8.0, 'L0_gnn_W_time': 8.0}
    for name, (base, spread) in spreads.items():
        noise = np.random.default_rng([zlib.crc32(name.encode()), seed]).standard_normal(out[name].shape)
        drawn = base * np.exp(spread * noise) if base else spread * noise
        out[name] = jnp.asarray(drawn.astype(out[name].dtype))
    for name, factor in factors.items():
        out[name] = (out[name] * factor).astype(out[name].dtype)
    return out
```

```python
from contextlib import ExitStack

import concourse.bass as bass
import numpy as np
from concourse import mybir

P = 128


class Steps:

    def __init__(self):
        self.value_of = {}
        self.counts = {}
        self.queues = {}

    def engine(self, name, own_sem):
        queue = []
        self.queues[name] = queue

        def do(emit, needs=(), mark=None, sem=None):
            at = own_sem if sem is None else sem
            by = 1 if sem is None else 16
            signalled = mark is not None
            if signalled:
                self.counts[at] = self.counts.get(at, 0) + by
                assert mark not in self.value_of, mark
                self.value_of[mark] = (at, self.counts[at])
            queue.append((needs, emit, at if signalled else None, by))

        return do

    def emit(self, name, engine):
        seen = {}
        for needs, emit, sem, by in self.queues[name]:
            for need in needs:
                at, value = self.value_of[need]
                if seen.get(at, 0) < value:
                    engine.wait_ge(at, value)
                    seen[at] = value
            ins = emit(engine)
            if sem is not None:
                ins.then_inc(sem, by)


def weight_columns(d, a, ed, sh1, sh2, e, h1, h2, out):
    k = d // P
    return {
        "wd": (P, (k, a)), "wt": (ed + 1, (a,)), "wf_node": (a, (a,)), "wf_time": (a, (a,)), "wu": (a + 1, (d,)),
        "w1": (P, (k, sh1)), "w2": (P, (k, sh2)), "w3": (P, (out,)), "we1": (P, (e, k, h1)), "we2": (P, (e, h2)),
        "we3": (P, (e // 2, out)), "b3": (e + 1, (out,)), "wg": (P, (k, e)), "bg": (1, (e,)),
        "b_d": (a, (1,)), "b_f": (a, (1,)), "b_1": (P, (k,)), "b_2": (P, (1,)), "b_e1": (P, (e,)), "b_e2": (P, (e // 2,)),
    }


def gnn_ffn(nc, x, src_t, attr_t, weights, dims, out):
    f32, bf16, i32 = mybir.dt.float32, mybir.dt.bfloat16, mybir.dt.int32
    ALU, ACT, AX = mybir.AluOpType, mybir.ActivationFunctionType, mybir.AxisListType

    N, D = x.shape
    ET = src_t.shape[1]
    D, A, ED, SH1, SH2, E_, H1, H2, OUT = dims
    NT = -(-N // P)
    TG = 5
    EG = ET // TG
    assert TG * NT <= 512 and ET % TG == 0
    LG = 3
    NL = -(-EG // LG)
    R = 2
    CH = R * P
    SH = CH.bit_length() - 1
    NCH = ET * P // CH + NT
    CL = 8
    NCL = -(-NCH // CL)
    NCH = NCL * CL
    ONE, MID, LOW, LO, ROW = A, A + 1, 2 * A + 1, 3 * A + 1, 3 * A + 2
    SW = A + 1
    Z = 64
    TN = 4
    NG = -(-NT // TN)
    K = D // P
    assert (A, D, H1, H2, E_, SH1, SH2, OUT) == (64, 256, 128, 64, 4, 256, 128, 256)
    EPS = 1e-5
    nt = [min(TN, NT - TN * g) for g in range(NG)]
    rows = [[min(P, N - (TN * g + t) * P) for t in range(nt[g])] for g in range(NG)]

    table = nc.dram_tensor("table", (NCH * CH, ROW), bf16, kind="Internal").ap()
    x_ln = nc.dram_tensor("x_ln", (NG * P, TN * D), f32, kind="Internal").ap()

    with ExitStack() as ctx:
        def sb(name, shape, dt):
            return ctx.enter_context(nc.sbuf_tensor(name, shape, dt))

        def sem(name):
            return ctx.enter_context(nc.semaphore(name))

        s_pe, s_dve, s_act, s_pool = sem("s_pe"), sem("s_dve"), sem("s_act"), sem("s_pool")
        s_w, s_src, s_zero_tail, s_zero_ends = sem("s_w"), sem("s_src"), sem("s_zero_tail"), sem("s_zero_ends")
        NA, NP, NTB = 3, 6, 3
        s_attr = [sem(f"s_attr{i}") for i in range(NA)]
        s_scatter = [sem(f"s_scatter{i}") for i in range(NP)]
        s_table = [sem(f"s_table{i}") for i in range(NTB)]
        s_x = [sem(f"s_x{i}") for i in range(2)]
        s_xln = [sem(f"s_xln{i}") for i in range(2)]
        s_xln_in = [sem(f"s_xln_in{i}") for i in range(2)]
        s_out = [sem(f"s_out{i}") for i in range(2)]

        w_all = sb("w_all", list(weights.shape), f32)
        views, at = {}, 0
        for name, (used, shape) in weight_columns(*dims).items():
            free = int(np.prod(shape))
            v = w_all[0:used, at:at + free]
            at += free
            if len(shape) > 1:
                names = "abc"[:len(shape)]
                v = v.rearrange(f"p ({' '.join(names)}) -> p {' '.join(names)}", **dict(zip(names[1:], shape[1:])))
            views[name] = v
        wd, wf_node, wf_time = views["wd"], views["wf_node"], views["wf_time"]
        wt = views["wt"]
        wu = views["wu"]
        w1, w2, w3, wg, bg = views["w1"], views["w2"], views["w3"], views["wg"], views["bg"]
        we1, we2 = views["we1"], views["we2"]
        we3 = views["we3"]
        b3 = views["b3"]
        b_d, b_f, b_1, b_2 = views["b_d"], views["b_f"], views["b_1"], views["b_2"]
        b_e1, b_e2 = views["b_e1"], views["b_e2"]
        iota_row = sb("iota_row", [P, P], f32)
        iota_col = sb("iota_col", [P, 1], f32)
        iota_bf = sb("iota_bf", [P, P], bf16)
        iota_wide = sb("iota_wide", [P, P, CL * R], bf16)
        ident = sb("ident", [P, P], f32)
        before = sb("before", [P, P], bf16)
        notbefore = sb("notbefore", [P, P], bf16)
        ones_bf = sb("ones_bf", [P, P], bf16)
        ones = sb("ones", [P, P], f32)
        eps_col = sb("eps_col", [P, 1], f32)
        first_rank = sb("first_rank", [P, E_], f32)
        sums_all = sb("sums", [P, max(NT * SW, Z * ROW // 2)], f32)
        sums = sums_all[:, 0:NT * SW]
        fused_node = sb("fused_node", [A, NG * TN * P], f32)
        offs = sb("offs", [1, NCH], i32)

        ARENA = 26500
        arena = sb("arena", [P, ARENA], f32)
        top = [0]

        def carve(shape, dt, partitions=P):
            free = int(np.prod(shape))
            words = free if dt != bf16 else (free + 1) // 2
            a = arena[0:partitions, top[0]:top[0] + words]
            top[0] += words
            assert top[0] <= ARENA, top[0]
            if dt != f32:
                a = a.bitcast(dt)[:, 0:free]
            if len(shape) == 1:
                return a
            names = "abcd"[:len(shape)]
            return a.rearrange(f"p ({' '.join(names)}) -> p {' '.join(names)}",
                               **dict(zip(names[1:], shape[1:])))

        src_i = carve([ET], i32)
        hi = carve([ET], bf16)
        lo = carve([ET], bf16)
        thr = carve([NT], f32)
        ge_count = carve([NT + 1], f32)
        tot = carve([NT + 1], f32)
        n_i = carve([NT], i32)
        c_i = carve([NT], i32)
        n_chunks = carve([NT], f32)
        end_chunk = carve([NT], f32)
        first_chunk = carve([NT], f32)
        last_chunk = carve([NT], f32)
        zeros_row = carve([NT], f32)
        base = carve([NT], f32)
        chunk_col = carve([2], f32)
        zero_idx = carve([CH // Z], i32)
        iota_chunk = carve([NCH], f32)
        started = carve([NCH], bf16)
        attr = [carve([LG * TG * P], f32, ED + 1) for _ in range(NA)]
        pay = [carve([TG, ROW], bf16) for _ in range(NP)]
        pos = [carve([TG], i32) for _ in range(NP)]
        onehot = [carve([TG, NT], bf16) for _ in range(2)]
        picked = carve([TG, NT], f32)
        rest = [carve([TG, A], f32) for _ in range(2)]
        shared_from = top[0]
        hi_i = carve([ET], i32)
        lo_i = carve([ET], i32)
        junk_v = [carve([ET], bf16) for _ in range(3)]
        junk_a = [carve([ET], bf16) for _ in range(3)]
        used_0 = top[0]
        top[0] = shared_from
        xa = [carve([TN, D], f32) for _ in range(2)]
        xn_a = carve([TN, D], f32)
        xs_a = carve([TN, D], f32)
        xt_a = carve([K, TN * P], f32)
        nf_a = carve([TN * P], f32, A)
        stat_a = carve([TN, 6], f32)
        mv_a = carve([TN, 2], f32)
        sd_a = carve([TN], f32)
        rs_a = carve([TN], f32)
        used_1 = max(top[0], used_0)
        top[0] = 0
        tab = [carve([CL, R, ROW], bf16) for _ in range(NTB)]
        hot = [carve([P, CL * R], bf16) for _ in range(2)]
        tab_lo = [carve([CL, R], bf16) for _ in range(2)]
        sums_odd = carve([NT * SW], f32)
        used_2 = top[0]
        top[0] = 0
        cnt = carve([TN], f32)
        rcnt = carve([TN], f32)
        ntf = carve([TN, A], f32)
        ntf_t = carve([TN * P], f32, A)
        pre = carve([TN * P], f32, A)
        fused = carve([TN * P], f32, A + 1)
        xs = [carve([TN, D], f32) for _ in range(2)]
        x1 = [carve([TN, D], f32) for _ in range(2)]
        xn = carve([TN, D], f32)
        stat = carve([TN, 6], f32)
        mv = carve([TN, 2], f32)
        var_eps = carve([TN], f32)
        minus_half = carve([TN], f32)
        rs = carve([TN], f32)
        yt = carve([K, TN * P], f32)
        h1 = carve([K, TN * P], f32)
        h2 = carve([TN * P], f32)
        e1 = carve([E_, TN * P], f32)
        e2r = carve([2, TN * P], f32)
        e2 = carve([2, TN * P], f32)
        lg = carve([TN, E_], f32)
        gm = carve([TN], f32)
        ge = carve([TN, E_], f32)
        sel1 = carve([TN, E_], f32)
        sel2 = carve([TN, E_], f32)
        sc = carve([TN, E_], f32)
        m1 = carve([TN], f32)
        m2 = carve([TN], f32)
        mt = carve([TN], f32)
        wa = carve([TN], f32)
        wb = carve([TN], f32)
        w5 = carve([TN, E_ + 1], f32)
        w_wide = carve([TN, E_ // 2, 2 * H2], f32)
        w5_t = carve([TN * P], f32, E_ + 1)
        o = [carve([TN, D], f32) for _ in range(2)]

        bank = [ctx.enter_context(nc.psum_tensor(f"bank{i}", [P, 512], f32)) for i in range(8)]

        steps = Steps()
        sp = steps.engine("sp", None)
        pe = steps.engine("pe", s_pe)
        dve = steps.engine("dve", s_dve)
        act = steps.engine("act", s_act)
        pool = steps.engine("pool", s_pool)

        def b3d(a, n, m):
            return a.unsqueeze(2).to_broadcast([a.shape[0], n, m])

        def b3r(a, n, m):
            return a.unsqueeze(1).to_broadcast([a.shape[0], n, m])

        sp(lambda e: e.dma_start(src_i, src_t), mark="src", sem=s_src)
        sp(lambda e: e.dma_start(w_all[:], weights), mark="weights", sem=s_w)

        def load_attr(n):
            first, m = n * LG, min(LG, EG - n * LG)
            needs = [("feat", (n - NA) * LG + LG - 1)] if n >= NA else ["attr_ones"]
            sp(lambda e: e.dma_start(attr[n % NA][0:ED, 0:m * TG * P],
                                     attr_t[:, first * TG * P:(first + m) * TG * P]),
               needs, ("attr", n), s_attr[n % NA])

        dve(lambda e: e.memset(sums_all[:], 0.0), mark="zeros")
        for a in attr:
            dve(lambda e, a=a: e.memset(a[ED:ED + 1, :], 1.0), mark=("attr_ones_", id(a)))
        dve(lambda e: e.memset(ones_bf[:], 1.0), mark="attr_ones")
        dve(lambda e: e.memset(ones[:], 1.0))
        dve(lambda e: e.memset(eps_col[:], EPS))
        dve(lambda e: e.memset(zeros_row, 0.0))
        dve(lambda e: e.memset(ge_count[:, 0:1], float(ET)))
        dve(lambda e: e.memset(ge_count[:, NT:NT + 1], 0.0))
        for q in pay:
            dve(lambda e, q=q: e.memset(q[:, :, ONE:ONE + 1], 1.0))
        pool(lambda e: e.iota(iota_row[:], pattern=[[1, P]], base=0, channel_multiplier=0,
                              allow_small_or_imprecise_dtypes=True))
        pool(lambda e: e.iota(iota_bf[:], pattern=[[1, P]], base=0, channel_multiplier=0,
                              allow_small_or_imprecise_dtypes=True))
        pool(lambda e: e.iota(iota_col[:], pattern=[[0, 1]], base=0, channel_multiplier=1,
                              allow_small_or_imprecise_dtypes=True))
        pool(lambda e: e.iota(first_rank[:], pattern=[[-1, E_]], base=E_, channel_multiplier=0,
                              allow_small_or_imprecise_dtypes=True))
        pool(lambda e: e.iota(iota_chunk, pattern=[[1, NCH]], base=0, channel_multiplier=0,
                              allow_small_or_imprecise_dtypes=True), mark="iota")
        dve(lambda e: e.tensor_scalar(thr, iota_row[:, 0:NT], -1.0, 0.5, ALU.mult, ALU.add), ["iota"], "thr")
        dve(lambda e: e.tensor_copy(iota_wide[:], b3d(iota_bf[:], P, CL * R)))
        dve(lambda e: e.tensor_scalar(before[:], iota_row[:], iota_col[:, 0:1], None, ALU.is_gt))
        dve(lambda e: e.tensor_scalar(notbefore[:], iota_row[:], iota_col[:, 0:1], None, ALU.is_le))
        dve(lambda e: e.tensor_scalar(ident[:], iota_row[:], iota_col[:, 0:1], None, ALU.is_equal), mark="const")

        tail = ET * P
        zsrc = sums_all[:].bitcast(bf16)
        for n, r0 in enumerate(range(tail, NCH * CH, P * Z)):
            m = min(P * Z, NCH * CH - r0)
            q, left = m // Z, m % Z
            for c0, cn, w in ((r0, q, Z), (r0 + q * Z, 1, left)):
                if cn and w:
                    sp(lambda e, c0=c0, cn=cn, w=w: e.dma_start(
                        table[c0:c0 + cn * w, :].rearrange("(p r) c -> p (r c)", r=w), zsrc[0:cn, 0:w * ROW]),
                       ["zeros"], ("tail", c0), s_zero_tail)
                    steps.value_of["tail"] = steps.value_of[("tail", c0)]
        for n in range(min(NA, NL)):
            load_attr(n)

        dve(lambda e: e.tensor_scalar(hi_i, src_i, 7, None, ALU.arith_shift_right), ["src"], "hi_i")
        dve(lambda e: e.tensor_copy(hi, hi_i), ["hi_i"], "hi")
        split = 1 + (NT - 1) * 55 // 100
        for c in range(1, split):
            act(lambda e, c=c: e.activation(junk_a[c % 3], hi, ACT.Sign, bias=thr[:, c:c + 1], accum_out=ge_count[:, c:c + 1]),
                ["hi", "thr"] + ([("sign", c - 3)] if c > 3 else []), ("sign", c))
        for c in range(split, NT):
            dve(lambda e, c=c: e.tensor_scalar(junk_v[c % 3], hi, float(c), None, ALU.is_ge, ALU.add, accum_out=ge_count[:, c:c + 1]),
                ["hi"] + ([("ge", c - 3)] if c >= split + 3 else []), ("ge", c))
        dve(lambda e: e.tensor_scalar(lo_i, src_i, 127, None, ALU.bitwise_and), (), "lo_i")
        dve(lambda e: e.tensor_copy(lo, lo_i), ["lo_i"], "lo")
        dve(lambda e: e.tensor_scalar(ge_count[:, 1:split], ge_count[:, 1:split], float(ET), 0.5, ALU.add, ALU.mult),
            [("sign", split - 1)], "ge_count")
        pe(lambda e: e.matmul(bank[1][:, 0:NT + 1], ones[:], ge_count, start=True, stop=True), ["ge_count", ("ge", NT - 1), "const"], "tot_ps")
        dve(lambda e: e.tensor_copy(tot, bank[1][:, 0:NT + 1]), ["tot_ps"], "tot")
        dve(lambda e: e.tensor_tensor(n_i, tot[:, 0:NT], tot[:, 1:NT + 1], ALU.subtract), ["tot"], "n_i")
        dve(lambda e: e.tensor_scalar(c_i, n_i, SH, None, ALU.arith_shift_right), ["n_i"], "c_i")
        dve(lambda e: e.tensor_scalar(n_chunks, c_i, 1.0, None, ALU.add), ["c_i"], "n_chunks")
        dve(lambda e: e.tensor_tensor_scan(end_chunk, n_chunks, zeros_row, 0.0, ALU.add, ALU.add), ["n_chunks"], "end_chunk")
        dve(lambda e: e.tensor_tensor(first_chunk, end_chunk, n_chunks, ALU.subtract), ["end_chunk"], "first_chunk")
        dve(lambda e: e.tensor_scalar(last_chunk, end_chunk, -1.0, None, ALU.add), (), "last_chunk")
        dve(lambda e: e.tensor_scalar(base, first_chunk, float(CH), None, ALU.mult), ["first_chunk"], "base")
        pe(lambda e: e.matmul(bank[1][0:NT, 128:129], first_chunk[0:1, :], ones[0:1, 0:1], start=True, stop=True),
           ["first_chunk", "tot"])
        pe(lambda e: e.matmul(bank[1][0:NT, 129:130], last_chunk[0:1, :], ones[0:1, 0:1], start=True, stop=True),
           ["last_chunk"], "chunk_ps")
        dve(lambda e: e.tensor_copy(chunk_col[0:NT, :], bank[1][0:NT, 128:130]), ["chunk_ps"], "chunk_col")
        for r in range(CH // Z):
            dve(lambda e, r=r: e.tensor_scalar(zero_idx[0:NT, r:r + 1], chunk_col[0:NT, 1:2], float(CH // Z), float(r), ALU.mult, ALU.add),
                ["chunk_col"], ("zero_idx", r))
        zrows = table.rearrange("(n r) c -> n (r c)", r=Z)
        for r in range(CH // Z):
            pool(lambda e, r=r: e.indirect_dma_start(
                out=zrows, out_offset=bass.IndirectOffsetOnAxis(ap=zero_idx[0:NT, r:r + 1], axis=0),
                in_=zsrc[0:NT, 0:Z * ROW], in_offset=None, bounds_check=NCH * CH // Z - 1, oob_is_err=False),
                 [("zero_idx", r), "tail"], ("ends", r), s_zero_ends)
        ends = ("ends", CH // Z - 1)
        dve(lambda e: e.tensor_scalar(started[0:NT, :], iota_chunk[0:NT, :], chunk_col[0:NT, 0:1], None, ALU.is_ge),
            ["chunk_col"], "started")
        for n, c0 in enumerate(range(0, NCH, 512)):
            w = min(512, NCH - c0)
            pe(lambda e, c0=c0, w=w, n=n: e.matmul(bank[2 + n % 2][0:1, 0:w], ones_bf[0:NT, 0:1], started[0:NT, c0:c0 + w], start=True, stop=True),
               ["started"] + ([("offs", n - 2)] if n >= 2 else []), ("offs_ps", n))
            dve(lambda e, c0=c0, w=w, n=n: e.tensor_scalar(offs[0:1, c0:c0 + w], bank[2 + n % 2][0:1, 0:w], -1.0, float(SW), ALU.add, ALU.mult),
                [("offs_ps", n)], ("offs", n))
        last_offs = ("offs", (NCH - 1) // 512)

        places = bank[0][:, 0:TG * NT]
        places3 = places.rearrange("p (j b) -> p j b", j=TG)
        pe(lambda e: e.matmul(places, ones[0:1, :], b3r(base[0:1, :], TG, NT), start=True, stop=True, skip_group_check=True),
           ["base"])

        def feat_ps(g):
            return bank[1 + g % 2][:, 0:TG * A].rearrange("p (j a) -> p j a", j=TG)

        def free(g):
            return [("scattered", g - NP)] if g >= NP else []

        def bucket_onehot(g):
            dve(lambda e: e.tensor_tensor(onehot[g % 2], b3r(iota_bf[:, 0:NT], TG, NT), b3d(hi[:, g * TG:(g + 1) * TG], TG, NT), ALU.is_equal),
                [("counted", g - 2)] if g >= 2 else ["hi"], ("onehot", g))

        def features(g):
            for j in range(TG):
                t = (g % LG) * TG + j
                pe(lambda e, j=j, t=t: e.matmul(feat_ps(g)[:, j, :], attr[g // LG % NA][:, t * P:(t + 1) * P], wt, start=True, stop=True),
                   [("attr", g // LG), "weights", last_offs] + ([("rest", g - 2)] if g >= 2 else []), ("feat", g) if j == TG - 1 else None)

        def find_places(g):
            hot_g = onehot[g % 2]
            pe(lambda e: e.matmul(places, before[:], hot_g.rearrange("p j b -> p (j b)"), start=False, stop=True, skip_group_check=True), [("onehot", g), "const"])
            for i in range(TG - 1):
                pe(lambda e, i=i: e.matmul(places3[:, i + 1:TG, :], ones_bf[:], b3r(hot_g[:, i, :], TG - 1 - i, NT), start=False, stop=True, skip_group_check=True),
                   (), ("places", g) if i == TG - 2 else None)
            dve(lambda e: e.tensor_tensor(picked, places3, hot_g, ALU.mult), [("places", g)] + ([("pos", g - 1)] if g else []), ("picked", g))

            def reduce_places(e):
                with nc.allow_low_precision(reason="one whole number below 2^24 and zeros: exact"):
                    return e.tensor_reduce(pos[g % NP], picked, AX.X, ALU.add)
            dve(reduce_places, [("picked", g)] + free(g), ("pos", g))

        def count_group(g):
            hot_g = onehot[g % 2]
            pe(lambda e: e.matmul(places, notbefore[:], hot_g.rearrange("p j b -> p (j b)"), start=False, stop=True, skip_group_check=True), [("picked", g)])
            for i in range(1, TG):
                pe(lambda e, i=i: e.matmul(places3[:, 0:i, :], ones_bf[:], b3r(hot_g[:, i, :], i, NT), start=False, stop=True, skip_group_check=True),
                   (), ("counted", g) if i == TG - 1 else None)

        def part_high(g):
            q = pay[g % NP]
            act(lambda e: e.activation(q[:, :, 0:A], feat_ps(g), ACT.Relu), [("feat", g)] + free(g), ("high", g))
            act(lambda e: e.activation(q[:, :, LO], lo[:, g * TG:(g + 1) * TG], ACT.Copy), ["lo"], ("lo", g))
            dve(lambda e: e.scalar_tensor_tensor(rest[g % 2], feat_ps(g), 0.0, q[:, :, 0:A], ALU.max, ALU.subtract),
                [("high", g)] + ([("low", g - 2)] if g >= 2 else []), ("rest", g))

        def part_mid(g):
            act(lambda e: e.activation(pay[g % NP][:, :, MID:MID + A], rest[g % 2], ACT.Copy), [("rest", g)], ("mid", g))

        def part_low(g):
            q = pay[g % NP]
            dve(lambda e: e.tensor_tensor(q[:, :, LOW:LOW + A], rest[g % 2], q[:, :, MID:MID + A], ALU.subtract),
                [("mid", g)], ("low", g))

        def scatter(g):
            q = g % NP
            for j in range(TG):
                pool(lambda e, j=j: e.indirect_dma_start(
                    out=table, out_offset=bass.IndirectOffsetOnAxis(ap=pos[q][:, j:j + 1], axis=0),
                    in_=pay[q][:, j, :], in_offset=None, bounds_check=NCH * CH - 1, oob_is_err=False),
                     [("low", g), ("pos", g), ("lo", g), ends],
                     ("scattered", g) if j == TG - 1 else ("scattering", g, j), s_scatter[q])

        edge_stages = [(2, count_group), (0, bucket_onehot), (1, find_places), (0, features), (3, part_low), (1, part_high),
                       (2, part_mid), (3, scatter)]
        BEHIND = max(lag for lag, _ in edge_stages)

        def node_first(a):
            n, w = nt[a], nt[a] * P
            xg, xb = xa[a % 2], x[a * TN * P:min((a + 1) * TN * P, N), :]

            def load():
                full = sum(r == P for r in rows[a])
                needs = [("xn_a", a - 2), ("xs_a", a - 2)] if a >= 2 else ["lo", ("sign", split - 1), ("ge", NT - 1)]
                if full:
                    sp(lambda e: e.dma_start(xg[:, 0:full, :], xb[0:full * P, :].rearrange("(t p) d -> p t d", p=P)), needs, ("x_full", a), s_x[a % 2])
                if full < n:
                    sp(lambda e: e.dma_start(xg[0:rows[a][-1], full, :], xb[full * P:, :]), needs, ("x_part", a), s_x[a % 2])
                steps.value_of[("x", a)] = steps.value_of[("x_part" if full < n else "x_full", a)]

            def stats():
                for t in range(n):
                    dve(lambda e, t=t: e.bn_stats(stat_a[:, t, :], xg[:, t, :]), [("x", a)], ("stat_a", a, t))
                for t in range(n):
                    dve(lambda e, t=t: e.bn_aggr(mv_a[:, t, :], stat_a[:, t, :]), [("stat_a", a, t)] + ([("xn_a", a - 1)] if a else []), ("mv_a", a, t))

            def root():
                act(lambda e: e.activation(sd_a[:, 0:n], mv_a[:, 0:n, 1], ACT.Sqrt, bias=eps_col[:]), [("mv_a", a, n - 1)], ("sd_a", a))

            def normed():
                dve(lambda e: e.reciprocal(rs_a[:, 0:n], sd_a[:, 0:n]), [("sd_a", a)], ("rs_a", a))
                for t in range(n):
                    dve(lambda e, t=t: e.tensor_scalar(xn_a[:, t, :], xg[:, t, :], mv_a[:, t, 0:1], rs_a[:, t:t + 1], ALU.subtract, ALU.mult),
                        [("rs_a", a)] + ([("xt_ps", a - 1), ("xs_a", a - 1)] if a else []), ("xn_a", a) if t == n - 1 else None)
                dve(lambda e: e.tensor_tensor(xs_a[:, 0:n, :], xg[:, 0:n, :], xn_a[:, 0:n, :], ALU.add),
                    [("xn_a", a)] + ([("x_ln", a - 1)] if a else []), ("xs_a", a))
                sp(lambda e: e.dma_start(x_ln[a * P:(a + 1) * P, 0:n * D], xs_a[:, 0:n, :].rearrange("p t d -> p (t d)")),
                   [("xs_a", a)], ("x_ln", a), s_xln[a % 2])

            def transposes():
                for k in range(K):
                    for t in range(n):
                        pe(lambda e, k=k, t=t: e.transpose(bank[3 + k][:, t * P:(t + 1) * P], xn_a[:, t, k * P:(k + 1) * P], ident[:]),
                           [("xn_a", a)] + ([("xt_a", a - 1)] if a else []), ("xt_ps", a) if (k, t) == (K - 1, n - 1) else None)

            def evacuate():
                for k in range(K):
                    act(lambda e, k=k: e.activation(xt_a[:, k, 0:w], bank[3 + k][:, 0:w], ACT.Copy),
                        [("xt_ps", a)], ("xt_a", a) if k == K - 1 else None)

            def down():
                for k in range(K):
                    pe(lambda e, k=k: e.matmul(bank[5][0:A, 0:w], wd[:, k, :], xt_a[:, k, 0:w], start=k == 0, stop=k == K - 1),
                       [("xt_a", a)], ("down", a) if k == K - 1 else None)

            def down_relu():
                act(lambda e: e.activation(nf_a[:, 0:w], bank[5][0:A, 0:w], ACT.Relu, bias=b_d), [("down", a)], ("nf_a", a))

            def fuse():
                pe(lambda e: e.matmul(bank[6][0:A, 0:w], wf_node, nf_a[:, 0:w], start=True, stop=True), [("nf_a", a)], ("fuse", a))

            def keep():
                act(lambda e: e.activation(fused_node[:, a * TN * P:a * TN * P + w], bank[6][0:A, 0:w], ACT.Identity, bias=b_f),
                    [("fuse", a)], ("fused_node", a))

            return [load, lambda: None, stats, root, normed, transposes, evacuate, down, down_relu, fuse, keep]

        period = max(EG // (NG + 1), 1)
        at_group = {}
        for a in range(NG):
            for k, step in enumerate(node_first(a)):
                at_group.setdefault(a * max(period, 11) + k, []).append(step)
        for g in range(max(EG + BEHIND, max(at_group) + 1)):
            for lag, stage in edge_stages:
                if 0 <= g - lag < EG:
                    stage(g - lag)
            if g % LG == 0 and g and g // LG + NA - 1 < NL:
                load_attr(g // LG + NA - 1)
            for step in at_group.get(g, []):
                step()
        scatter_done = [("scattered", g) for g in range(max(0, EG - NP), EG)]
        first_half_done = [("fused_node", NG - 1)] + [("x_ln", a) for a in range(max(0, NG - 2), NG)]

        def load_table(n):
            needs = [("sum_ps", n - NTB)] if n >= NTB else scatter_done + first_half_done + [("low", EG - 1), ("counted", EG - 1), ("feat", EG - 1)]
            sp(lambda e: e.dma_start(tab[n % NTB], table[n * CL * CH:(n + 1) * CL * CH, :].rearrange("(c p r) w -> p c r w", p=P, r=R)),
               needs, ("tab", n), s_table[n % NTB])

        def make_hot(n):
            two = n % 2
            dve(lambda e: e.tensor_copy(tab_lo[two], tab[n % NTB][:, :, :, LO]), [("tab", n)] + ([("hot", n - 2)] if n >= 2 else []), ("tab_lo", n))
            dve(lambda e: e.tensor_tensor(hot[two], iota_wide[:], b3r(tab_lo[two].rearrange("p c r -> p (c r)"), P, CL * R), ALU.is_equal),
                [("tab_lo", n)] + ([("sum_ps", n - 2)] if n >= 2 else []), ("hot", n))

        def add_up(n):
            for c in range(CL):
                ps = bank[4 * (n % 2) + c // 4][:, (c % 4) * SW:(c % 4 + 1) * SW]
                for i, (r, c0, w) in enumerate([(r, c0, w) for r in range(R) for c0, w in ((0, SW), (MID, A), (LOW, A))]):
                    pe(lambda e, c=c, ps=ps, i=i, r=r, c0=c0, w=w: e.matmul(ps[:, 0:w], hot[n % 2][:, :, c * R + r], tab[n % NTB][:, c, r, c0:c0 + w],
                                                                            start=i == 0, stop=i == 3 * R - 1),
                       [("hot", n)] + ([("added", n - 2, CL - 1)] if n >= 2 else []), ("sum_ps", n) if (c, i) == (CL - 1, 3 * R - 1) else None)

        regs = []

        def add_in(n):
            at_of = [None] * CL
            for c in range(CL):
                def emit(e, c=c):
                    if not regs:
                        regs.extend(e.alloc_register(f"column{i}") for i in range(CL))
                    if c == 0:
                        e.reg_load(regs, offs[0:1, n * CL:(n + 1) * CL])
                        at_of[:] = [e.snap(r, min_val=0, max_val=(NT - 1) * SW) for r in regs]
                    d = (sums, sums_odd)[c % 2][:, bass.ds(at_of[c], SW)]
                    return e.tensor_tensor(d, d, bank[4 * (n % 2) + c // 4][:, (c % 4) * SW:(c % 4 + 1) * SW], ALU.add)
                before_it = ("added", n, c - 2) if c >= 2 else (("added", n - 1, CL - 2 + c) if n else "odd_zeros")
                dve(emit, [("sum_ps", n), before_it], ("added", n, c))

        for n in range(NCL):
            load_table(n)
            make_hot(n)
            if n == 0:
                dve(lambda e: e.memset(sums_odd, 0.0), mark="odd_zeros")
            add_up(n)
            if n:
                add_in(n - 1)
        add_in(NCL - 1)
        dve(lambda e: e.tensor_tensor(sums, sums, sums_odd, ALU.add), [("added", NCL - 1, CL - 1), ("added", NCL - 1, CL - 2)], "summed")
        summed = "summed"

        BX, BO, BH, BS, BG = (0, 1), (2, 3), (4, 5), 6, 7
        dve(lambda e: e.memset(minus_half, -0.5), [summed], "minus_half")
        dve(lambda e: e.memset(w5[:, :, E_:E_ + 1], 1.0))
        dve(lambda e: e.memset(fused[A:A + 1, :], 1.0), mark="fused_one")

        def half(i, t):
            return bank[i[t // 2]][:, (t % 2) * D:(t % 2 + 1) * D]

        def prev(name, g, back=1):
            return [(name, g - back)] if g >= back else []

        def load_xs(g):
            sp(lambda e: e.dma_start(xs[g % 2][:, 0:nt[g], :].rearrange("p t d -> p (t d)"), x_ln[g * P:(g + 1) * P, 0:nt[g] * D]),
               [summed] + prev("x1", g, 2), ("xs", g), s_xln_in[g % 2])

        def light_mean(g):
            n = nt[g]
            s3 = sums[:, g * TN * SW:(g * TN + n) * SW].rearrange("p (t c) -> p t c", c=SW)
            dve(lambda e: e.tensor_scalar(cnt[:, 0:n], s3[:, :, A], 1.0, None, ALU.max), [summed], ("cnt", g))
            dve(lambda e: e.reciprocal(rcnt[:, 0:n], cnt[:, 0:n]), [("cnt", g)], ("rcnt", g))
            dve(lambda e: e.tensor_tensor(ntf[:, 0:n, :], s3[:, :, 0:A], b3d(rcnt[:, 0:n], n, A), ALU.mult),
                [("rcnt", g)] + prev("ntf_ps", g), ("ntf", g))

        def light_mean_t(g):
            n = nt[g]
            for t in range(n):
                pe(lambda e, t=t: e.transpose(bank[BS][0:A, t * P:(t + 1) * P], ntf[:, t, :], ident[:]),
                   [("ntf", g)] + prev("pre", g), ("ntf_ps", g) if t == n - 1 else None)
            act(lambda e: e.activation(ntf_t[:, 0:n * P], bank[BS][0:A, 0:n * P], ACT.Copy), [("ntf_ps", g)], ("ntf_t", g))

        def light_fuse(g):
            w = nt[g] * P
            pe(lambda e: e.matmul(bank[BS][0:A, 0:w], wf_time, ntf_t[:, 0:w], start=True, stop=True), [("ntf_t", g)], ("fuse_ps", g))
            dve(lambda e: e.tensor_tensor(pre[:, 0:w], bank[BS][0:A, 0:w], fused_node[:, g * TN * P:g * TN * P + w], ALU.add),
                [("fuse_ps", g)] + prev("fused", g), ("pre", g))
            act(lambda e: e.activation(fused[0:A, 0:w], pre[:, 0:w], ACT.Relu), [("pre", g)], ("fused", g))

        def light_up(g):
            n = nt[g]
            xq = x1[g % 2]
            for t in range(n):
                pe(lambda e, t=t: e.matmul(half(BX, t), fused[:, t * P:(t + 1) * P], wu, start=True, stop=True),
                   [("fused", g), "fused_one"] + prev("yt", g), ("up", g) if t == n - 1 else None)
            for t in range(0, n, 2):
                m = min(2, n - t)
                dve(lambda e, t=t, m=m: e.tensor_tensor(xq[:, t:t + m, :].rearrange("p t d -> p (t d)"), xs[g % 2][:, t:t + m, :].rearrange("p t d -> p (t d)"),
                                                        bank[BX[t // 2]][:, 0:m * D], ALU.add),
                    [("up", g), ("xs", g)] + prev("o", g, 2), ("x1", g) if t + 2 >= n else ("x1a", g))
            for t in range(n):
                dve(lambda e, t=t: e.bn_stats(stat[:, t, :], xq[:, t, :]), [("x1", g)], ("stat", g, t))
            for t in range(n):
                dve(lambda e, t=t: e.bn_aggr(mv[:, t, :], stat[:, t, :]), [("stat", g, t)] + prev("xn", g), ("mv", g, t))
            dve(lambda e: e.tensor_scalar(var_eps[:, 0:n], mv[:, 0:n, 1], EPS, None, ALU.add), [("mv", g, n - 1)], ("var_eps", g))
            pool(lambda e: e.tensor_tensor(rs[:, 0:n], var_eps[:, 0:n], minus_half[:, 0:n], ALU.pow), [("var_eps", g), "minus_half"] + prev("xn", g), ("rs", g))
            for t in range(n):
                dve(lambda e, t=t: e.tensor_scalar(xn[:, t, :], xq[:, t, :], mv[:, t, 0:1], rs[:, t:t + 1], ALU.subtract, ALU.mult),
                    [("rs", g)] + prev("y_ps", g), ("xn", g) if t == n - 1 else None)

        def light_y_t(g):
            n = nt[g]
            for k in range(K):
                for t in range(n):
                    pe(lambda e, k=k, t=t: e.transpose(bank[BX[k]][:, t * P:(t + 1) * P], xn[:, t, k * P:(k + 1) * P], ident[:]),
                       [("xn", g)], ("y_ps", g) if (k, t) == (K - 1, n - 1) else None)
            for k in range(K):
                act(lambda e, k=k: e.activation(yt[:, k, 0:n * P], bank[BX[k]][:, 0:n * P], ACT.Copy), [("y_ps", g)], ("yt", g) if k == K - 1 else None)

        def light_gate(g):
            n = nt[g]
            gp = bank[BG][:, 0:n * E_]
            for t in range(n):
                at = gp[:, t * E_:(t + 1) * E_]
                for k in range(K):
                    pe(lambda e, k=k, t=t, at=at: e.matmul(at, yt[:, k, t * P:(t + 1) * P], wg[:, k, :], start=k == 0, stop=False),
                       [("yt", g)] + prev("mul1", g))
                pe(lambda e, at=at: e.matmul(at, ones[0:1, :], bg, start=False, stop=True), (), ("gate_ps", g) if t == n - 1 else None)
            g3 = gp.rearrange("p (t c) -> p t c", c=E_)
            dve(lambda e: e.tensor_reduce(gm[:, 0:n], g3, AX.X, ALU.max), [("gate_ps", g)], ("gm", g))
            dve(lambda e: e.tensor_tensor(lg[:, 0:n, :], g3, b3d(gm[:, 0:n], n, E_), ALU.subtract), [("gm", g)], ("lg", g))
            act(lambda e: e.activation(ge[:, 0:n, :], lg[:, 0:n, :], ACT.Exp), [("lg", g)], ("ge", g))

        def light_top2(g):
            n = nt[g]
            last = [("ge", g)]
            at = [0]

            def link(emit):
                at[0] += 1
                dve(emit, [last[0]], ("top", g, at[0]))
                last[0] = ("top", g, at[0])
            v = lambda a: a[:, 0:n, :]
            c = lambda a: b3d(a[:, 0:n], n, E_)
            link(lambda e: e.tensor_reduce(m1[:, 0:n], v(ge), AX.X, ALU.add))
            link(lambda e: e.reciprocal(m2[:, 0:n], m1[:, 0:n]))
            link(lambda e: e.tensor_tensor(v(ge), v(ge), c(m2), ALU.mult))

            def pick(m, sel):
                link(lambda e: e.tensor_reduce(m[:, 0:n], v(ge), AX.X, ALU.max))
                link(lambda e: e.tensor_tensor(v(sc), v(ge), c(m), ALU.is_equal))
                link(lambda e: e.tensor_tensor(v(sc), v(sc), b3r(first_rank[:], n, E_), ALU.mult))
                link(lambda e: e.tensor_reduce(mt[:, 0:n], v(sc), AX.X, ALU.max))
                link(lambda e: e.tensor_tensor(v(sel), v(sc), c(mt), ALU.is_equal))
            pick(m1, sel1)
            link(lambda e: e.scalar_tensor_tensor(v(ge), v(sel1), -2.0, v(ge), ALU.mult, ALU.add))
            pick(m2, sel2)
            link(lambda e: e.tensor_tensor(mt[:, 0:n], m2[:, 0:n], m1[:, 0:n], ALU.subtract))
            act(lambda e: e.activation(wb[:, 0:n], mt[:, 0:n], ACT.Exp), [last[0]], ("e2", g))
            last[0] = ("e2", g)
            link(lambda e: e.tensor_scalar(mt[:, 0:n], wb[:, 0:n], 1.0, None, ALU.add))
            link(lambda e: e.reciprocal(wa[:, 0:n], mt[:, 0:n]))
            link(lambda e: e.tensor_tensor(wb[:, 0:n], wb[:, 0:n], wa[:, 0:n], ALU.mult))
            link(lambda e: e.tensor_tensor(v(sel1), v(sel1), c(wa), ALU.mult))
            link(lambda e: e.tensor_tensor(v(sel2), v(sel2), c(wb), ALU.mult))
            dve(lambda e: e.tensor_tensor(w5[:, 0:n, 0:E_], v(sel1), v(sel2), ALU.add), [last[0]], ("w5", g))
            for t in range(n):
                pool(lambda e, t=t: e.tensor_copy(w_wide[:, t, :, :].rearrange("p q (e j) -> p (q e) j", j=H2), b3d(w5[:, t, 0:E_], E_, H2)),
                     [("w5", g)] + prev("spread1", g), ("w_wide", g) if t == n - 1 else None)

        uses = [0]

        def hidden(g, name, out_sb, parts, bias, needs):
            w = nt[g] * P
            u = uses[0]
            uses[0] += 1
            b = bank[BH[u % 2]]
            for i, (po, pn, lhs, rhs, first, final) in enumerate(parts):
                pe(lambda e, po=po, pn=pn, lhs=lhs, rhs=rhs, first=first, final=final: e.matmul(b[po:po + pn, 0:w], lhs, rhs, start=first, stop=final),
                   needs + ([("hid", u - 2)] if u >= 2 else []), ("hid_ps", u) if i == len(parts) - 1 else None)
            act(lambda e: e.activation(out_sb, b[:, 0:w], ACT.Relu, bias=bias), [("hid_ps", u)], ("hid", u))
            steps.value_of[(name, g)] = steps.value_of[("hid", u)]

        def shared1(g, m):
            w = nt[g] * P
            hidden(g, f"h1_{m}", h1[:, m, 0:w], [(0, P, w1[:, k, m * P:(m + 1) * P], yt[:, k, 0:w], k == 0, k == K - 1) for k in range(K)],
                   b_1[:, m:m + 1], [("yt", g)])

        def shared2(g):
            w = nt[g] * P
            hidden(g, "h2", h2[:, 0:w], [(0, P, w2[:, k, :], h1[:, k, 0:w], k == 0, k == K - 1) for k in range(K)], b_2, [("h1_0", g), ("h1_1", g)])

        def expert1(g, x_):
            w = nt[g] * P
            hidden(g, f"e1_{x_}", e1[:, x_, 0:w], [(0, P, we1[:, x_, k, :], yt[:, k, 0:w], k == 0, k == K - 1) for k in range(K)],
                   b_e1[:, x_:x_ + 1], [("yt", g)])

        def expert2(g, q):
            w = nt[g] * P
            hidden(g, f"e2_{q}", e2r[:, q, 0:w], [(i * H2, H2, we2[:, 2 * q + i, :], e1[:, 2 * q + i, 0:w], True, True) for i in range(2)],
                   b_e2[:, q:q + 1], [(f"e1_{2 * q}", g), (f"e1_{2 * q + 1}", g)])

        def weights_t(g):
            n = nt[g]
            for t in range(n):
                pe(lambda e, t=t: e.transpose(bank[BG][0:E_ + 1, t * P:(t + 1) * P], w5[:, t, :], ident[:]),
                   [("w5", g)], ("w5_ps", g) if t == n - 1 else None)
            act(lambda e: e.activation(w5_t[:, 0:n * P], bank[BG][0:E_ + 1, 0:n * P], ACT.Copy), [("w5_ps", g)], ("w5_t", g))

        def spread(g, q):
            n = nt[g]
            for t in range(n):
                pe(lambda e, t=t: e.transpose(bank[BG][:, t * P:(t + 1) * P], w_wide[:, t, q, :], ident[:]),
                   [("w5_t", g) if q == 0 else ("mul0", g), ("w_wide", g)], (f"spread{q}", g) if t == n - 1 else None)
            dve(lambda e: e.tensor_tensor(e2[:, q, 0:n * P], e2r[:, q, 0:n * P], bank[BG][:, 0:n * P], ALU.mult),
                [(f"spread{q}", g), (f"e2_{q}", g)] + prev("out_ps", g), (f"mul{q}", g))

        def final(g, part):
            n = nt[g]
            if part == 0:
                terms = [(h2, w3, ("h2", g)), (w5_t, b3, ("w5_t", g)), (e2[:, 0, :], we3[:, 0, :], ("mul0", g))]
            else:
                terms = [(e2[:, 1, :], we3[:, 1, :], ("mul1", g))]
            for t in range(n):
                for i, (lhs, rhs, need) in enumerate(terms):
                    pe(lambda e, t=t, i=i, lhs=lhs, rhs=rhs: e.matmul(half(BO, t), lhs[:, t * P:(t + 1) * P], rhs, start=part == 0 and i == 0 and t % 2 == 0,
                                                                      stop=part == 1, skip_group_check=True),
                       [need] + (prev("o", g) if part == 0 else []), ("out_ps", g) if (part, t) == (1, n - 1) else None)

        def finish(g):
            n = nt[g]
            for t in range(0, n, 2):
                m = min(2, n - t)
                dve(lambda e, t=t, m=m: e.tensor_tensor(o[g % 2][:, t:t + m, :].rearrange("p t d -> p (t d)"), x1[g % 2][:, t:t + m, :].rearrange("p t d -> p (t d)"),
                                                        bank[BO[t // 2]][:, 0:m * D], ALU.add),
                    [("out_ps", g)] + prev("stored", g, 2), ("o", g) if t + 2 >= n else None)
            full = sum(r == P for r in rows[g])
            r0 = g * TN * P
            if full:
                sp(lambda e: e.dma_start(out[r0:r0 + full * P, :].rearrange("(t p) d -> p t d", p=P), o[g % 2][:, 0:full, :]),
                   [("o", g)], ("stored_full", g), s_out[g % 2])
            if full < n:
                sp(lambda e: e.dma_start(out[r0 + full * P:N, :], o[g % 2][0:rows[g][-1], full, :]), [("o", g)], ("stored_part", g), s_out[g % 2])
            steps.value_of[("stored", g)] = steps.value_of[("stored_part" if full < n else "stored_full", g)]

        load_xs(0)
        for i in range(NG + 1):
            heavy, light = i - 1 if i else None, i if i < NG else None
            both = [
                (heavy, lambda g: shared1(g, 0)), (heavy, lambda g: shared1(g, 1)),
                (light, light_mean), (light, light_mean_t), (heavy, weights_t),
                (heavy, lambda g: expert1(g, 0)), (light, light_fuse), (heavy, shared2),
                (light, light_up), (heavy, lambda g: expert1(g, 1)), (heavy, lambda g: expert1(g, 2)),
                (heavy, lambda g: expert2(g, 0)), (heavy, lambda g: spread(g, 0)),
                (heavy, lambda g: expert1(g, 3)), (heavy, lambda g: final(g, 0)),
                (heavy, lambda g: expert2(g, 1)), (heavy, lambda g: spread(g, 1)),
                (light, light_y_t), (light, light_gate), (heavy, lambda g: final(g, 1)),
                (light, light_top2), (heavy, finish),
            ]
            if i + 1 < NG:
                load_xs(i + 1)
            for g, step in both:
                if g is not None:
                    step(g)

        def wait_outputs(e):
            for g in range(max(0, NG - 2), NG):
                at, value = steps.value_of[("stored", g)]
                e.wait_ge(at, value)

        with nc.Block() as block:
            @block.sync
            def _(e):
                steps.emit("sp", e)
                wait_outputs(e)

            @block.tensor
            def _(e):
                steps.emit("pe", e)

            @block.vector
            def _(e):
                steps.emit("dve", e)

            @block.scalar
            def _(e):
                steps.emit("act", e)

            @block.gpsimd
            def _(e):
                steps.emit("pool", e)


def kernel(**inputs):
    import concourse.bacc as bacc
    from concourse.bass_utils import run_bass_kernel_spmd

    a = {k: np.asarray(v) for k, v in inputs.items()}
    n, d = a["x"].shape
    edges, ed = a["edge_attr_32"].shape
    node_tiles = -(-n // P)
    tg = 5
    tiles = -(-edges // (P * tg)) * tg
    assert n < node_tiles * P
    src = np.full((tiles * P,), node_tiles * P - 1, np.int32)
    src[:edges] = a["src"]
    attr = np.zeros((ed, tiles * P), np.float32)
    attr[:, :edges] = a["edge_attr_32"].T
    g, f = "L0_gnn_", "L0_ffn_"

    def by_partition(w):
        return w.reshape(-1, P, w.shape[-1]).transpose(1, 0, 2)

    ew1, ew2, ew3 = a[f + "eW1"], a[f + "eW2"], a[f + "eW3"]
    e, _, h1 = ew1.shape
    h2 = ew2.shape[2]
    parts = {
        "wd": by_partition(a[g + "W_down"].T), "wt": np.vstack([a[g + "W_time"].T, a[g + "b_time"][None]]),
        "wf_node": a[g + "W_fusion"].T[:len(a[g + "b_down"])], "wf_time": a[g + "W_fusion"].T[len(a[g + "b_down"]):],
        "wu": np.vstack([a[g + "W_up"].T, a[g + "b_up"][None]]),
        "w1": by_partition(a[f + "sW1"]), "w2": by_partition(a[f + "sW2"]), "w3": a[f + "sW3"],
        "we1": ew1.reshape(e, -1, P, h1).transpose(2, 0, 1, 3), "we2": ew2.transpose(1, 0, 2),
        "we3": ew3.reshape(e // 2, 2 * h2, -1).transpose(1, 0, 2), "b3": np.vstack([a[f + "eb3"], a[f + "sb3"][None]]),
        "wg": by_partition(a[f + "gW"]), "bg": a[f + "gb"][None],
        "b_d": a[g + "b_down"][:, None], "b_f": a[g + "b_fusion"][:, None],
        "b_1": a[f + "sb1"].reshape(-1, P).T, "b_2": a[f + "sb2"][:, None],
        "b_e1": a[f + "eb1"].T, "b_e2": a[f + "eb2"].reshape(e // 2, -1).T,
    }
    dims = (d, len(a[g + "b_down"]), ed, a[f + "sW1"].shape[1], a[f + "sW2"].shape[1], e, h1, h2, ew3.shape[2])
    columns = weight_columns(*dims)
    weights = np.zeros((P, sum(int(np.prod(shape)) for _, shape in columns.values())), np.float32)
    at = 0
    for name, (used, shape) in columns.items():
        free = int(np.prod(shape))
        weights[:used, at:at + free] = parts[name].reshape(used, free)
        at += free
    given = [("x", a["x"]), ("src_t", src.reshape(tiles, P).T), ("attr_t", attr), ("weights", weights)]

    nc = bacc.Bacc("TRN2", target_bir_lowering=False, num_devices=1)
    arrays, args = {}, []
    for name, v in given:
        v = np.ascontiguousarray(v)
        arrays[f"in_{name}"] = v
        args.append(nc.dram_tensor(f"in_{name}", v.shape, mybir.dt.from_np(v.dtype), kind="ExternalInput").ap())
    args.append(nc.dram_tensor("out_rows", (n, d), mybir.dt.float32, kind="ExternalOutput").ap())
    gnn_ffn(nc, *args[:-1], dims, args[-1])
    return run_bass_kernel_spmd(nc, [arrays], core_ids=[0]).results[0]["out_rows"]
```

```python
from contextlib import ExitStack

import concourse.bass as bass
import numpy as np
from concourse import mybir

P = 128


class Steps:

    def __init__(self):
        self.value_of = {}
        self.counts = {}
        self.queues = {}

    def engine(self, name, own_sem):
        queue = []
        self.queues[name] = queue

        def do(emit, needs=(), mark=None, sem=None):
            at = own_sem if sem is None else sem
            by = 1 if sem is None else 16
            signalled = mark is not None
            if signalled:
                self.counts[at] = self.counts.get(at, 0) + by
                assert mark not in self.value_of, mark
                self.value_of[mark] = (at, self.counts[at])
            queue.append((needs, emit, at if signalled else None, by))

        return do

    def emit(self, name, engine):
        seen = {}
        for needs, emit, sem, by in self.queues[name]:
            for need in needs:
                at, value = self.value_of[need]
                if seen.get(at, 0) < value:
                    engine.wait_ge(at, value)
                    seen[at] = value
            ins = emit(engine)
            if sem is not None:
                ins.then_inc(sem, by)


def weight_columns(d, a, ed, sh1, sh2, e, h1, h2, out):
    k = d // P
    return {
        "wd": (P, (k, a)), "wt": (ed + 1, (a,)), "wf_node": (a, (a,)), "wf_time": (a, (a,)), "wu": (a + 1, (d,)),
        "w1": (P, (k, sh1)), "w2": (P, (k, sh2)), "w3": (P, (out,)), "we1": (P, (e, k, h1)), "we2": (P, (e, h2)),
        "we3": (P, (e // 2, out)), "b3": (e + 1, (out,)), "wg": (P, (k, e)), "bg": (P, (e,)),
        "b_d": (a, (1,)), "b_f": (a, (1,)), "b_1": (P, (k,)), "b_2": (P, (1,)), "b_e1": (P, (e,)), "b_e2": (P, (e // 2,)),
    }


def gnn_ffn(nc, x, src_t, attr_t, weights, dims, out):
    f32, bf16, i32 = mybir.dt.float32, mybir.dt.bfloat16, mybir.dt.int32
    ALU, ACT, AX = mybir.AluOpType, mybir.ActivationFunctionType, mybir.AxisListType

    N, D = x.shape
    ET = src_t.shape[1]
    D, A, ED, SH1, SH2, E_, H1, H2, OUT = dims
    NT = -(-N // P)
    TG = 5
    EG = ET // TG
    assert TG * NT <= 512 and ET % TG == 0
    LG = 3
    NL = -(-EG // LG)
    R = 2
    CH = R * P
    SH = CH.bit_length() - 1
    CL = 8
    SHARES = (45, 35, 20)
    cuts = [0]
    for share in SHARES[:-1]:
        cuts.append(cuts[-1] + max(LG, EG * share // 100 // LG * LG))
    cuts.append(EG)
    parts = [(cuts[k], cuts[k + 1]) for k in range(len(SHARES))]
    part_of = [k for k, (g0, g1) in enumerate(parts) for _ in range(g0, g1)]
    loads = [-(-((g1 - g0) * TG * P // CH + NT) // CL) for g0, g1 in parts]
    n_ch = [n * CL for n in loads]
    offs_at = [sum(n_ch[:k]) for k in range(len(parts))]
    PT = max(g1 - g0 for g0, g1 in parts) * TG
    ONE, MID, LOW, LO, ROW = A, A + 1, 2 * A + 1, 3 * A + 1, 3 * A + 2
    SW = A + 1
    Z = 64
    TN = 4
    NG = -(-NT // TN)
    K = D // P
    assert (A, D, H1, H2, E_, SH1, SH2, OUT) == (64, 256, 128, 64, 4, 256, 128, 256)
    EPS = 1e-5
    nt = [min(TN, NT - TN * g) for g in range(NG)]
    rows = [[min(P, N - (TN * g + t) * P) for t in range(nt[g])] for g in range(NG)]

    tables = [nc.dram_tensor(f"table{k}", (n * CH, ROW), bf16, kind="Internal").ap() for k, n in enumerate(n_ch)]
    fused_dram = nc.dram_tensor("fused_node", (NG * A, TN * P), f32, kind="Internal").ap()
    x_ln = nc.dram_tensor("x_ln", (NG * P, TN * D), f32, kind="Internal").ap()

    with ExitStack() as ctx:
        def sb(name, shape, dt):
            return ctx.enter_context(nc.sbuf_tensor(name, shape, dt))

        def sem(name):
            return ctx.enter_context(nc.semaphore(name))

        s_pe, s_dve, s_act, s_pool = sem("s_pe"), sem("s_dve"), sem("s_act"), sem("s_pool")
        s_w, s_src, s_zero_tail, s_zero_ends = sem("s_w"), sem("s_src"), sem("s_zero_tail"), sem("s_zero_ends")
        NA, NP, NTB = 3, 6, 3
        s_attr = [sem(f"s_attr{i}") for i in range(NA)]
        s_scatter = [sem(f"s_scatter{i}") for i in range(NP)]
        s_fused = [sem(f"s_fused{i}") for i in range(2)]
        s_fused_in = [sem(f"s_fused_in{i}") for i in range(2)]
        s_table = [sem(f"s_table{i}") for i in range(NTB)]
        s_x = [sem(f"s_x{i}") for i in range(2)]
        s_xln = [sem(f"s_xln{i}") for i in range(2)]
        s_xln_in = [sem(f"s_xln_in{i}") for i in range(2)]
        s_out = [sem(f"s_out{i}") for i in range(2)]

        w_all = sb("w_all", list(weights.shape), f32)
        views, at = {}, 0
        for name, (used, shape) in weight_columns(*dims).items():
            free = int(np.prod(shape))
            v = w_all[0:used, at:at + free]
            at += free
            if len(shape) > 1:
                names = "abc"[:len(shape)]
                v = v.rearrange(f"p ({' '.join(names)}) -> p {' '.join(names)}", **dict(zip(names[1:], shape[1:])))
            views[name] = v
        wd, wf_node, wf_time = views["wd"], views["wf_node"], views["wf_time"]
        wt = views["wt"]
        wu = views["wu"]
        w1, w2, w3, wg, bg = views["w1"], views["w2"], views["w3"], views["wg"], views["bg"]
        we1, we2 = views["we1"], views["we2"]
        we3 = views["we3"]
        b3 = views["b3"]
        b_d, b_f, b_1, b_2 = views["b_d"], views["b_f"], views["b_1"], views["b_2"]
        b_e1, b_e2 = views["b_e1"], views["b_e2"]
        iota_row = sb("iota_row", [P, P], f32)
        iota_col = sb("iota_col", [P, 1], f32)
        iota_bf = sb("iota_bf", [P, P], bf16)
        iota_wide = sb("iota_wide", [P, P, CL * R], bf16)
        ident = sb("ident", [P, P], f32)
        before = sb("before", [P, P], bf16)
        notbefore = sb("notbefore", [P, P], bf16)
        ones_bf = sb("ones_bf", [P, P], bf16)
        ones = sb("ones", [P, P], f32)
        eps_col = sb("eps_col", [P, 1], f32)
        first_rank = sb("first_rank", [P, E_], f32)
        sums_all = sb("sums", [P, max(NT * SW, Z * ROW // 2)], f32)
        sums = sums_all[:, 0:NT * SW]
        offs = sb("offs", [1, sum(n_ch)], i32)

        ARENA = 39000
        arena = sb("arena", [P, ARENA], f32)
        top = [0]

        def carve(shape, dt, partitions=P):
            free = int(np.prod(shape))
            words = free if dt != bf16 else (free + 1) // 2
            a = arena[0:partitions, top[0]:top[0] + words]
            top[0] += words
            assert top[0] <= ARENA, top[0]
            if dt != f32:
                a = a.bitcast(dt)[:, 0:free]
            if len(shape) == 1:
                return a
            names = "abcd"[:len(shape)]
            return a.rearrange(f"p ({' '.join(names)}) -> p {' '.join(names)}",
                               **dict(zip(names[1:], shape[1:])))

        src_i = carve([ET], i32)
        hi = carve([ET], bf16)
        lo = carve([ET], bf16)
        thr = carve([NT], f32)
        ge_count = carve([NT + 1], f32)
        tot = carve([NT + 1], f32)
        n_i = carve([NT], i32)
        c_i = carve([NT], i32)
        n_chunks = carve([NT], f32)
        end_chunk = carve([NT], f32)
        first_chunk = carve([NT], f32)
        last_chunk = carve([NT], f32)
        zeros_row = carve([NT], f32)
        base = [carve([NT], f32) for _ in parts]
        chunk_col = carve([2], f32)
        zero_idx = carve([CH // Z], i32)
        iota_chunk = carve([max(n_ch)], f32)
        started = carve([max(n_ch)], bf16)
        attr = [carve([LG * TG * P], f32, ED + 1) for _ in range(NA)]
        pay = [carve([TG, ROW], bf16) for _ in range(NP)]
        pos = [carve([TG], i32) for _ in range(NP)]
        onehot = [carve([TG, NT], bf16) for _ in range(2)]
        picked = carve([TG, NT], f32)
        rest = [carve([TG, A], f32) for _ in range(2)]
        tab = [carve([CL, R, ROW], bf16) for _ in range(NTB)]
        hot = [carve([P, CL * R], bf16) for _ in range(2)]
        tab_lo = [carve([CL, R], bf16) for _ in range(2)]
        sums_odd = carve([NT * SW], f32)
        junk_v = [carve([PT], bf16) for _ in range(3)]
        junk_a = [carve([PT], bf16) for _ in range(3)]
        shared_from = top[0]
        hi_i = carve([ET], i32)
        lo_i = carve([ET], i32)
        used_0 = top[0]
        top[0] = shared_from
        xa = [carve([TN, D], f32) for _ in range(2)]
        xn_a = carve([TN, D], f32)
        xs_a = carve([TN, D], f32)
        xt_a = carve([K, TN * P], f32)
        nf_a = carve([TN * P], f32, A)
        fused_a = [carve([TN * P], f32, A) for _ in range(2)]
        stat_a = carve([TN, 6], f32)
        mv_a = carve([TN, 2], f32)
        sd_a = carve([TN], f32)
        rs_a = carve([TN], f32)
        used_1 = max(top[0], used_0)
        top[0] = 0
        cnt = carve([TN], f32)
        rcnt = carve([TN], f32)
        ntf = carve([TN, A], f32)
        ntf_t = carve([TN * P], f32, A)
        fused_in = [carve([TN * P], f32, A) for _ in range(2)]
        pre = carve([TN * P], f32, A)
        fused = carve([TN * P], f32, A + 1)
        xs = [carve([TN, D], f32) for _ in range(2)]
        x1 = [carve([TN, D], f32) for _ in range(2)]
        xn = carve([TN, D], f32)
        stat = carve([TN, 6], f32)
        mv = carve([TN, 2], f32)
        var_eps = carve([TN], f32)
        minus_half = carve([TN], f32)
        rs = carve([TN], f32)
        yt = carve([K, TN * P], f32)
        h1 = carve([K, TN * P], f32)
        h2 = carve([TN * P], f32)
        e1 = carve([E_, TN * P], f32)
        e2r = carve([2, TN * P], f32)
        e2 = carve([2, TN * P], f32)
        lg = carve([TN, E_], f32)
        gm = carve([TN], f32)
        ge = carve([TN, E_], f32)
        sel1 = carve([TN, E_], f32)
        sel2 = carve([TN, E_], f32)
        sc = carve([TN, E_], f32)
        m1 = carve([TN], f32)
        m2 = carve([TN], f32)
        mt = carve([TN], f32)
        wa = carve([TN], f32)
        wb = carve([TN], f32)
        w5 = carve([TN, E_ + 1], f32)
        w_wide = carve([TN, E_ // 2, 2 * H2], f32)
        w5_t = carve([TN * P], f32, E_ + 1)
        o = [carve([TN, D], f32) for _ in range(2)]
        assert max(used_1, top[0]) <= ARENA, (used_1, top[0])

        bank = [ctx.enter_context(nc.psum_tensor(f"bank{i}", [P, 512], f32)) for i in range(8)]

        steps = Steps()
        sp = steps.engine("sp", None)
        pe = steps.engine("pe", s_pe)
        dve = steps.engine("dve", s_dve)
        act = steps.engine("act", s_act)
        pool = steps.engine("pool", s_pool)

        def b3d(a, n, m):
            return a.unsqueeze(2).to_broadcast([a.shape[0], n, m])

        def b3r(a, n, m):
            return a.unsqueeze(1).to_broadcast([a.shape[0], n, m])

        sp(lambda e: e.dma_start(src_i, src_t), mark="src", sem=s_src)
        sp(lambda e: e.dma_start(w_all[:], weights), mark="weights", sem=s_w)

        def load_attr(n):
            first, m = n * LG, min(LG, EG - n * LG)
            needs = [("feat", (n - NA) * LG + LG - 1)] if n >= NA else ["attr_ones"]
            sp(lambda e: e.dma_start(attr[n % NA][0:ED, 0:m * TG * P],
                                     attr_t[:, first * TG * P:(first + m) * TG * P]),
               needs, ("attr", n), s_attr[n % NA])

        dve(lambda e: e.memset(sums_all[:], 0.0), mark="zeros")
        for a in attr:
            dve(lambda e, a=a: e.memset(a[ED:ED + 1, :], 1.0), mark=("attr_ones_", id(a)))
        dve(lambda e: e.memset(ones_bf[:], 1.0), mark="attr_ones")
        dve(lambda e: e.memset(ones[:], 1.0))
        dve(lambda e: e.memset(eps_col[:], EPS))
        dve(lambda e: e.memset(zeros_row, 0.0))
        dve(lambda e: e.memset(ge_count[:, NT:NT + 1], 0.0))
        dve(lambda e: e.memset(sums_odd, 0.0))
        for q in pay:
            dve(lambda e, q=q: e.memset(q[:, :, ONE:ONE + 1], 1.0))
        pool(lambda e: e.iota(iota_row[:], pattern=[[1, P]], base=0, channel_multiplier=0,
                              allow_small_or_imprecise_dtypes=True))
        pool(lambda e: e.iota(iota_bf[:], pattern=[[1, P]], base=0, channel_multiplier=0,
                              allow_small_or_imprecise_dtypes=True))
        pool(lambda e: e.iota(iota_col[:], pattern=[[0, 1]], base=0, channel_multiplier=1,
                              allow_small_or_imprecise_dtypes=True))
        pool(lambda e: e.iota(first_rank[:], pattern=[[-1, E_]], base=E_, channel_multiplier=0,
                              allow_small_or_imprecise_dtypes=True))
        pool(lambda e: e.iota(iota_chunk, pattern=[[1, max(n_ch)]], base=0, channel_multiplier=0,
                              allow_small_or_imprecise_dtypes=True), mark="iota")
        dve(lambda e: e.tensor_scalar(thr, iota_row[:, 0:NT], -1.0, 0.5, ALU.mult, ALU.add), ["iota"], "thr")
        dve(lambda e: e.tensor_copy(iota_wide[:], b3d(iota_bf[:], P, CL * R)))
        dve(lambda e: e.tensor_scalar(before[:], iota_row[:], iota_col[:, 0:1], None, ALU.is_gt))
        dve(lambda e: e.tensor_scalar(notbefore[:], iota_row[:], iota_col[:, 0:1], None, ALU.is_le))
        dve(lambda e: e.tensor_scalar(ident[:], iota_row[:], iota_col[:, 0:1], None, ALU.is_equal), mark="const")

        zsrc = sums_all[:].bitcast(bf16)
        for k, (g0, g1) in enumerate(parts):
            for r0 in range((g1 - g0) * TG * P, n_ch[k] * CH, P * Z):
                m = min(P * Z, n_ch[k] * CH - r0)
                q, left = m // Z, m % Z
                for c0, cn, w in ((r0, q, Z), (r0 + q * Z, 1, left)):
                    if cn and w:
                        sp(lambda e, k=k, c0=c0, cn=cn, w=w: e.dma_start(
                            tables[k][c0:c0 + cn * w, :].rearrange("(p r) c -> p (r c)", r=w), zsrc[0:cn, 0:w * ROW]),
                           ["zeros"], ("tail", k, c0), s_zero_tail)
                        steps.value_of["tail"] = steps.value_of[("tail", k, c0)]
        for n in range(min(NA, NL)):
            load_attr(n)

        dve(lambda e: e.tensor_scalar(hi_i, src_i, 7, None, ALU.arith_shift_right), ["src"], "hi_i")
        dve(lambda e: e.tensor_copy(hi, hi_i), ["hi_i"], "hi")
        dve(lambda e: e.tensor_scalar(lo_i, src_i, 127, None, ALU.bitwise_and), (), "lo_i")
        dve(lambda e: e.tensor_copy(lo, lo_i), ["lo_i"], "lo")

        def tiles_of(k):
            return hi[:, parts[k][0] * TG:parts[k][1] * TG], (parts[k][1] - parts[k][0]) * TG

        def sign_count(k, c):
            h, n = tiles_of(k)
            act(lambda e: e.activation(junk_a[c % 3][:, 0:n], h, ACT.Sign, bias=thr[:, c:c + 1], accum_out=ge_count[:, c:c + 1]),
                ["hi", "thr"] + ([("sign", k, c - 3)] if c > 3 else []) + ([("tot_ps", k - 1)] if k else []), ("sign", k, c))

        def compare_count(k, c, first):
            h, n = tiles_of(k)
            dve(lambda e: e.tensor_scalar(junk_v[c % 3][:, 0:n], h, float(c), None, ALU.is_ge, ALU.add, accum_out=ge_count[:, c:c + 1]),
                ["hi"] + ([("ge", k, c - 3)] if c >= first + 3 else []), ("ge", k, c))

        def sizes(k, split):
            n = tiles_of(k)[1]
            ps = bank[6]
            dve(lambda e: e.memset(ge_count[:, 0:1], float(n)), [("tot_ps", k - 1)] if k else [], ("ge_all", k))
            dve(lambda e: e.tensor_scalar(ge_count[:, 1:split], ge_count[:, 1:split], float(n), 0.5, ALU.add, ALU.mult),
                [("sign", k, split - 1)], ("ge_count", k))
            pe(lambda e: e.matmul(ps[:, 0:NT + 1], ones[:], ge_count, start=True, stop=True),
               [("ge_count", k), "const"] + last_read[6] + ([("ge", k, NT - 1)] if split < NT else []), ("tot_ps", k))
            dve(lambda e: e.tensor_copy(tot, ps[:, 0:NT + 1]), [("tot_ps", k)], ("tot", k))
            dve(lambda e: e.tensor_tensor(n_i, tot[:, 0:NT], tot[:, 1:NT + 1], ALU.subtract), [("tot", k)], ("n_i", k))
            dve(lambda e: e.tensor_scalar(c_i, n_i, SH, None, ALU.arith_shift_right), [("n_i", k)], ("c_i", k))
            dve(lambda e: e.tensor_scalar(n_chunks, c_i, 1.0, None, ALU.add), [("c_i", k)], ("n_chunks", k))
            dve(lambda e: e.tensor_tensor_scan(end_chunk, n_chunks, zeros_row, 0.0, ALU.add, ALU.add), [("n_chunks", k)], ("end_chunk", k))
            dve(lambda e: e.tensor_tensor(first_chunk, end_chunk, n_chunks, ALU.subtract), [("end_chunk", k)], ("first_chunk", k))
            dve(lambda e: e.tensor_scalar(last_chunk, end_chunk, -1.0, None, ALU.add), (), ("last_chunk", k))
            dve(lambda e: e.tensor_scalar(base[k], first_chunk, float(CH), None, ALU.mult), [("first_chunk", k)], ("base", k))
            pe(lambda e: e.matmul(ps[0:NT, 128:129], first_chunk[0:1, :], ones[0:1, 0:1], start=True, stop=True), [("first_chunk", k), ("tot", k)])
            pe(lambda e: e.matmul(ps[0:NT, 129:130], last_chunk[0:1, :], ones[0:1, 0:1], start=True, stop=True), [("last_chunk", k)], ("chunk_ps", k))
            dve(lambda e: e.tensor_copy(chunk_col[0:NT, :], ps[0:NT, 128:130]), [("chunk_ps", k)], ("chunk_col", k))
            last_read[6] = [("chunk_col", k)]
            for r in range(CH // Z):
                dve(lambda e, r=r: e.tensor_scalar(zero_idx[0:NT, r:r + 1], chunk_col[0:NT, 1:2], float(CH // Z), float(r), ALU.mult, ALU.add),
                    [("chunk_col", k)] + ([("ends", k - 1)] if k else []), ("zero_idx", k, r))
            zrows = tables[k].rearrange("(n r) c -> n (r c)", r=Z)
            for r in range(CH // Z):
                pool(lambda e, r=r: e.indirect_dma_start(
                    out=zrows, out_offset=bass.IndirectOffsetOnAxis(ap=zero_idx[0:NT, r:r + 1], axis=0),
                    in_=zsrc[0:NT, 0:Z * ROW], in_offset=None, bounds_check=n_ch[k] * CH // Z - 1, oob_is_err=False),
                     [("zero_idx", k, r), "tail"], ("ends", k) if r == CH // Z - 1 else ("end", k, r), s_zero_ends)
            dve(lambda e: e.tensor_scalar(started[0:NT, 0:n_ch[k]], iota_chunk[0:NT, 0:n_ch[k]], chunk_col[0:NT, 0:1], None, ALU.is_ge),
                [("chunk_col", k)], ("started", k))
            for i, c0 in enumerate(range(0, n_ch[k], 512)):
                w = min(512, n_ch[k] - c0)
                b = bank[7 - i % 2][0:1, 0:w]
                pe(lambda e, c0=c0, w=w, b=b: e.matmul(b, ones_bf[0:NT, 0:1], started[0:NT, c0:c0 + w], start=True, stop=True),
                   [("started", k)] + last_read[7 - i % 2], ("offs_ps", k, i))
                dve(lambda e, k=k, c0=c0, w=w, b=b: e.tensor_scalar(offs[0:1, offs_at[k] + c0:offs_at[k] + c0 + w], b, -1.0, float(SW), ALU.add, ALU.mult),
                    [("offs_ps", k, i)], ("offs", k, i))
                last_read[7 - i % 2] = [("offs", k, i)]
            steps.value_of[("sized", k)] = steps.value_of[("offs", k, (n_ch[k] - 1) // 512)]

        last_read = {6: [], 7: []}
        split = 1 + (NT - 1) * 50 // 100
        for c in range(1, split):
            sign_count(0, c)
        for c in range(split, NT):
            compare_count(0, c, split)
        sizes(0, split)

        places = bank[0][:, 0:TG * NT]
        places3 = places.rearrange("p (j b) -> p j b", j=TG)
        def feat_ps(g):
            return bank[1 + g % 2][:, 0:TG * A].rearrange("p (j a) -> p j a", j=TG)

        def free(g):
            return [("scattered", g - NP)] if g >= NP else []

        def bucket_onehot(g):
            dve(lambda e: e.tensor_tensor(onehot[g % 2], b3r(iota_bf[:, 0:NT], TG, NT), b3d(hi[:, g * TG:(g + 1) * TG], TG, NT), ALU.is_equal),
                [("counted", g - 2)] if g >= 2 else ["hi"], ("onehot", g))

        def features(g):
            for j in range(TG):
                t = (g % LG) * TG + j
                pe(lambda e, j=j, t=t: e.matmul(feat_ps(g)[:, j, :], attr[g // LG % NA][:, t * P:(t + 1) * P], wt, start=True, stop=True),
                   [("attr", g // LG), "weights", ("sized", 0)] + ([("rest", g - 2)] if g >= 2 else []), ("feat", g) if j == TG - 1 else None)

        def find_places(g):
            hot_g = onehot[g % 2]
            k = part_of[g]
            if g == parts[k][0]:
                pe(lambda e: e.matmul(places, ones[0:1, :], b3r(base[k][0:1, :], TG, NT), start=True, stop=True, skip_group_check=True),
                   [("base", k)] + ([("picked", g - 1)] if g else []), ("placed", k))
            pe(lambda e: e.matmul(places, before[:], hot_g.rearrange("p j b -> p (j b)"), start=False, stop=True, skip_group_check=True), [("onehot", g), "const"])
            for i in range(TG - 1):
                pe(lambda e, i=i: e.matmul(places3[:, i + 1:TG, :], ones_bf[:], b3r(hot_g[:, i, :], TG - 1 - i, NT), start=False, stop=True, skip_group_check=True),
                   (), ("places", g) if i == TG - 2 else None)
            dve(lambda e: e.tensor_tensor(picked, places3, hot_g, ALU.mult), [("places", g)] + ([("pos", g - 1)] if g else []), ("picked", g))

            def reduce_places(e):
                with nc.allow_low_precision(reason="one whole number below 2^24 and zeros: exact"):
                    return e.tensor_reduce(pos[g % NP], picked, AX.X, ALU.add)
            dve(reduce_places, [("picked", g)] + free(g), ("pos", g))

        def count_group(g):
            hot_g = onehot[g % 2]
            pe(lambda e: e.matmul(places, notbefore[:], hot_g.rearrange("p j b -> p (j b)"), start=False, stop=True, skip_group_check=True), [("picked", g)])
            for i in range(1, TG):
                pe(lambda e, i=i: e.matmul(places3[:, 0:i, :], ones_bf[:], b3r(hot_g[:, i, :], i, NT), start=False, stop=True, skip_group_check=True),
                   (), ("counted", g) if i == TG - 1 else None)

        def part_high(g):
            q = pay[g % NP]
            act(lambda e: e.activation(q[:, :, 0:A], feat_ps(g), ACT.Relu), [("feat", g)] + free(g), ("high", g))
            act(lambda e: e.activation(q[:, :, LO], lo[:, g * TG:(g + 1) * TG], ACT.Copy), ["lo"], ("lo", g))
            dve(lambda e: e.scalar_tensor_tensor(rest[g % 2], feat_ps(g), 0.0, q[:, :, 0:A], ALU.max, ALU.subtract),
                [("high", g)] + ([("low", g - 2)] if g >= 2 else []), ("rest", g))

        def part_mid(g):
            act(lambda e: e.activation(pay[g % NP][:, :, MID:MID + A], rest[g % 2], ACT.Copy), [("rest", g)], ("mid", g))

        def part_low(g):
            q = pay[g % NP]
            dve(lambda e: e.tensor_tensor(q[:, :, LOW:LOW + A], rest[g % 2], q[:, :, MID:MID + A], ALU.subtract),
                [("mid", g)], ("low", g))

        def scatter(g):
            q = g % NP
            k = part_of[g]
            for j in range(TG):
                pool(lambda e, j=j: e.indirect_dma_start(
                    out=tables[k], out_offset=bass.IndirectOffsetOnAxis(ap=pos[q][:, j:j + 1], axis=0),
                    in_=pay[q][:, j, :], in_offset=None, bounds_check=n_ch[k] * CH - 1, oob_is_err=False),
                     [("low", g), ("pos", g), ("lo", g), ("ends", k)],
                     ("scattered", g) if j == TG - 1 else ("scattering", g, j), s_scatter[q])

        edge_stages = [(2, count_group), (0, bucket_onehot), (1, find_places), (0, features), (3, part_low), (1, part_high),
                       (2, part_mid), (3, scatter)]
        BEHIND = max(lag for lag, _ in edge_stages)

        def node_first(a):
            n, w = nt[a], nt[a] * P
            xg, xb = xa[a % 2], x[a * TN * P:min((a + 1) * TN * P, N), :]

            def load():
                full = sum(r == P for r in rows[a])
                needs = [("xn_a", a - 2), ("xs_a", a - 2)] if a >= 2 else ["lo"]
                if full:
                    sp(lambda e: e.dma_start(xg[:, 0:full, :], xb[0:full * P, :].rearrange("(t p) d -> p t d", p=P)), needs, ("x_full", a), s_x[a % 2])
                if full < n:
                    sp(lambda e: e.dma_start(xg[0:rows[a][-1], full, :], xb[full * P:, :]), needs, ("x_part", a), s_x[a % 2])
                steps.value_of[("x", a)] = steps.value_of[("x_part" if full < n else "x_full", a)]

            def stats():
                for t in range(n):
                    dve(lambda e, t=t: e.bn_stats(stat_a[:, t, :], xg[:, t, :]), [("x", a)], ("stat_a", a, t))
                for t in range(n):
                    dve(lambda e, t=t: e.bn_aggr(mv_a[:, t, :], stat_a[:, t, :]), [("stat_a", a, t)] + ([("xn_a", a - 1)] if a else []), ("mv_a", a, t))

            def root():
                act(lambda e: e.activation(sd_a[:, 0:n], mv_a[:, 0:n, 1], ACT.Sqrt, bias=eps_col[:]), [("mv_a", a, n - 1)], ("sd_a", a))

            def normed():
                dve(lambda e: e.reciprocal(rs_a[:, 0:n], sd_a[:, 0:n]), [("sd_a", a)], ("rs_a", a))
                for t in range(n):
                    dve(lambda e, t=t: e.tensor_scalar(xn_a[:, t, :], xg[:, t, :], mv_a[:, t, 0:1], rs_a[:, t:t + 1], ALU.subtract, ALU.mult),
                        [("rs_a", a)] + ([("xt_ps", a - 1), ("xs_a", a - 1)] if a else []), ("xn_a", a) if t == n - 1 else None)
                dve(lambda e: e.tensor_tensor(xs_a[:, 0:n, :], xg[:, 0:n, :], xn_a[:, 0:n, :], ALU.add),
                    [("xn_a", a)] + ([("x_ln", a - 1)] if a else []), ("xs_a", a))
                sp(lambda e: e.dma_start(x_ln[a * P:(a + 1) * P, 0:n * D], xs_a[:, 0:n, :].rearrange("p t d -> p (t d)")),
                   [("xs_a", a)], ("x_ln", a), s_xln[a % 2])

            def transposes():
                for k in range(K):
                    for t in range(n):
                        pe(lambda e, k=k, t=t: e.transpose(bank[3 + k][:, t * P:(t + 1) * P], xn_a[:, t, k * P:(k + 1) * P], ident[:]),
                           [("xn_a", a)] + ([("xt_a", a - 1)] if a else []), ("xt_ps", a) if (k, t) == (K - 1, n - 1) else None)

            def evacuate():
                for k in range(K):
                    act(lambda e, k=k: e.activation(xt_a[:, k, 0:w], bank[3 + k][:, 0:w], ACT.Copy),
                        [("xt_ps", a)], ("xt_a", a) if k == K - 1 else None)

            def down():
                for k in range(K):
                    pe(lambda e, k=k: e.matmul(bank[5][0:A, 0:w], wd[:, k, :], xt_a[:, k, 0:w], start=k == 0, stop=k == K - 1),
                       [("xt_a", a)] + ([("fused_a", a - 1)] if a else []), ("down", a) if k == K - 1 else None)

            def down_relu():
                act(lambda e: e.activation(nf_a[:, 0:w], bank[5][0:A, 0:w], ACT.Relu, bias=b_d), [("down", a)], ("nf_a", a))

            def fuse():
                pe(lambda e: e.matmul(bank[5][0:A, 0:w], wf_node, nf_a[:, 0:w], start=True, stop=True), [("nf_a", a)], ("fuse", a))

            def keep():
                act(lambda e: e.activation(fused_a[a % 2][:, 0:w], bank[5][0:A, 0:w], ACT.Identity, bias=b_f),
                    [("fuse", a)] + ([("fused_kept", a - 2)] if a >= 2 else []), ("fused_a", a))

            def store():
                sp(lambda e: e.dma_start(fused_dram[a * A:(a + 1) * A, 0:w], fused_a[a % 2][:, 0:w]), [("fused_a", a)], ("fused_kept", a), s_fused[a % 2])

            return [load, lambda: None, stats, root, normed, transposes, evacuate, down, down_relu, fuse, keep, store]

        period = max(EG // (NG + 1), 1)
        at_group = {}
        for a in range(NG):
            for k, step in enumerate(node_first(a)):
                at_group.setdefault(a * max(period, 11) + k, []).append(step)
        room = max(1, parts[0][1] - 2 * NP - 4)
        per = -(-(NT - 1) * (len(parts) - 1) // room)
        at = NP
        for k in range(1, len(parts)):
            for c in range(1, NT, per):
                at_group.setdefault(at, []).append(lambda k=k, c=c: [sign_count(k, x_) for x_ in range(c, min(c + per, NT))])
                at += 1
            at_group.setdefault(at, []).append(lambda k=k: sizes(k, NT))
        all_zeroed = [("ends", len(parts) - 1)]

        regs = []
        hots = [0]

        def sum_steps(k):
            t0 = sum(loads[:k])
            banks = [6, 7] if k < len(parts) - 1 else [3, 4, 5, 6, 7]
            done = [("scattered", g) for g in range(max(0, parts[k][1] - NP), parts[k][1])]

            def load(n):
                t = t0 + n
                sp(lambda e: e.dma_start(tab[t % NTB], tables[k][n * CL * CH:(n + 1) * CL * CH, :].rearrange("(c p r) w -> p c r w", p=P, r=R)),
                   ([("sum_ps", t - NTB)] if t >= NTB else []) + (done if n == 0 else []), ("tab", t), s_table[t % NTB])

            def make_hot(n):
                t = t0 + n
                two = t % 2
                dve(lambda e: e.tensor_copy(tab_lo[two], tab[t % NTB][:, :, :, LO]), [("tab", t)] + ([("hot", t - 2)] if t >= 2 else []), ("tab_lo", t))
                dve(lambda e: e.tensor_tensor(hot[two], iota_wide[:], b3r(tab_lo[two].rearrange("p c r -> p (c r)"), P, CL * R), ALU.is_equal),
                    [("tab_lo", t)] + ([("sum_ps", t - 2)] if t >= 2 else []), ("hot", t))

            def ps_of(n, c):
                h = 2 * n + c // 4
                return bank[banks[h % len(banks)]][:, (c % 4) * SW:(c % 4 + 1) * SW], banks[h % len(banks)]

            def add_up(n):
                t = t0 + n
                for c in range(CL):
                    ps, b = ps_of(n, c)
                    needs = [("hot", t)] + (last_read[b] if c % 4 == 0 else [])
                    for i, (r, c0, w) in enumerate([(r, c0, w) for r in range(R) for c0, w in ((0, SW), (MID, A), (LOW, A))]):
                        pe(lambda e, c=c, ps=ps, i=i, r=r, c0=c0, w=w: e.matmul(ps[:, 0:w], hot[t % 2][:, :, c * R + r], tab[t % NTB][:, c, r, c0:c0 + w],
                                                                                start=i == 0, stop=i == 3 * R - 1),
                           needs, (("sum_ps", t) if c == CL - 1 else ("sum_ps4", t)) if (c % 4, i) == (3, 3 * R - 1) else None)
                    if c % 4 == 3:
                        last_read[b] = [("added", t, c)]

            def add_in(n):
                t = t0 + n
                at_of = [None] * CL
                for c in range(CL):
                    def emit(e, c=c):
                        if not regs:
                            regs.extend(e.alloc_register(f"column{i}") for i in range(CL))
                        if c == 0:
                            e.reg_load(regs, offs[0:1, t * CL:(t + 1) * CL])
                            at_of[:] = [e.snap(r, min_val=0, max_val=(NT - 1) * SW) for r in regs]
                        d = (sums, sums_odd)[c % 2][:, bass.ds(at_of[c], SW)]
                        return e.tensor_tensor(d, d, ps_of(n, c)[0], ALU.add)
                    before_it = [("added", t, c - 2)] if c >= 2 else ([("added", t - 1, CL - 2 + c)] if t else [])
                    dve(emit, [("sum_ps4", t) if c < 4 else ("sum_ps", t), ("sized", k)] + all_zeroed + before_it, ("added", t, c))

            return load, make_hot, add_up, add_in

        def sum_turns(k):
            load, make_hot, add_up, add_in = sum_steps(k)
            n_loads = loads[k]

            def before_products(n):
                if n == -1:
                    for m in range(min(NTB - 1, n_loads)):
                        load(m)
                if 0 <= n and n + NTB - 1 < n_loads:
                    load(n + NTB - 1)
                if n >= 1:
                    add_in(n - 1)
                if n + 1 < n_loads:
                    make_hot(n + 1)

            def products(n):
                if 0 <= n < n_loads:
                    add_up(n)
            return [(lambda n=n: before_products(n), lambda n=n: products(n)) for n in range(-1, n_loads + 1)]

        first_in_group, last_in_group = {}, {}
        for k in range(len(parts) - 1):
            g0, g1 = parts[k + 1]
            start = g0 + BEHIND + NP + 2
            turns = sum_turns(k)
            stop = g1 + BEHIND
            for i, (dve_half, pe_half) in enumerate(turns):
                g = start + i * (stop - start) // len(turns)
                first_in_group.setdefault(g, []).append(dve_half)
                last_in_group.setdefault(g, []).append(pe_half)

        for g in range(max(EG + BEHIND, max(at_group) + 1)):
            for step in first_in_group.get(g, []):
                step()
            for lag, stage in edge_stages:
                if 0 <= g - lag < EG:
                    stage(g - lag)
            if g % LG == 0 and g and g // LG + NA - 1 < NL:
                load_attr(g // LG + NA - 1)
            for step in at_group.get(g, []) + last_in_group.get(g, []):
                step()
        for b in (3, 4, 5):
            last_read[b] = [("fused_a", NG - 1), ("xt_a", NG - 1)]
        for dve_half, pe_half in sum_turns(len(parts) - 1):
            dve_half()
            pe_half()
        last = sum(loads) - 1
        dve(lambda e: e.tensor_tensor(sums, sums, sums_odd, ALU.add), [("added", last, CL - 1), ("added", last, CL - 2)], "summed")
        summed = "summed"
        first_half_done = [(name, a) for a in range(max(0, NG - 2), NG) for name in ("x_ln", "fused_kept")]

        BX, BO, BH, BS, BG = (0, 1), (2, 3), (4, 5), 6, 7
        dve(lambda e: e.memset(minus_half, -0.5), [summed], "minus_half")
        dve(lambda e: e.memset(w5[:, :, E_:E_ + 1], 1.0))
        dve(lambda e: e.memset(fused[A:A + 1, :], 1.0), mark="fused_one")

        def half(i, t):
            return bank[i[t // 2]][:, (t % 2) * D:(t % 2 + 1) * D]

        def prev(name, g, back=1):
            return [(name, g - back)] if g >= back else []

        def load_xs(g):
            sp(lambda e: e.dma_start(xs[g % 2][:, 0:nt[g], :].rearrange("p t d -> p (t d)"), x_ln[g * P:(g + 1) * P, 0:nt[g] * D]),
               [summed] + first_half_done + prev("x1", g, 2), ("xs", g), s_xln_in[g % 2])
            sp(lambda e: e.dma_start(fused_in[g % 2][:, 0:nt[g] * P], fused_dram[g * A:(g + 1) * A, 0:nt[g] * P]),
               prev("pre", g, 2), ("fused_in", g), s_fused_in[g % 2])

        def light_mean(g):
            n = nt[g]
            s3 = sums[:, g * TN * SW:(g * TN + n) * SW].rearrange("p (t c) -> p t c", c=SW)
            dve(lambda e: e.tensor_scalar(cnt[:, 0:n], s3[:, :, A], 1.0, None, ALU.max), [summed], ("cnt", g))
            dve(lambda e: e.reciprocal(rcnt[:, 0:n], cnt[:, 0:n]), [("cnt", g)], ("rcnt", g))
            dve(lambda e: e.tensor_tensor(ntf[:, 0:n, :], s3[:, :, 0:A], b3d(rcnt[:, 0:n], n, A), ALU.mult),
                [("rcnt", g)] + prev("ntf_ps", g), ("ntf", g))

        def light_mean_t(g):
            n = nt[g]
            for t in range(n):
                pe(lambda e, t=t: e.transpose(bank[BS][0:A, t * P:(t + 1) * P], ntf[:, t, :], ident[:]),
                   [("ntf", g)] + prev("logits", g), ("ntf_ps", g) if t == n - 1 else None)
            act(lambda e: e.activation(ntf_t[:, 0:n * P], bank[BS][0:A, 0:n * P], ACT.Copy), [("ntf_ps", g)], ("ntf_t", g))

        def light_fuse(g):
            w = nt[g] * P
            pe(lambda e: e.matmul(bank[BS][0:A, 0:w], wf_time, ntf_t[:, 0:w], start=True, stop=True), [("ntf_t", g)], ("fuse_ps", g))
            dve(lambda e: e.tensor_tensor(pre[:, 0:w], bank[BS][0:A, 0:w], fused_in[g % 2][:, 0:w], ALU.add),
                [("fuse_ps", g), ("fused_in", g)] + prev("fused", g), ("pre", g))
            act(lambda e: e.activation(fused[0:A, 0:w], pre[:, 0:w], ACT.Relu), [("pre", g)], ("fused", g))

        def light_up(g):
            n = nt[g]
            xq = x1[g % 2]
            for t in range(n):
                pe(lambda e, t=t: e.matmul(half(BX, t), fused[:, t * P:(t + 1) * P], wu, start=True, stop=True),
                   [("fused", g), "fused_one"] + prev("yt", g), ("up", g) if t == n - 1 else None)
            for t in range(0, n, 2):
                m = min(2, n - t)
                dve(lambda e, t=t, m=m: e.tensor_tensor(xq[:, t:t + m, :].rearrange("p t d -> p (t d)"), xs[g % 2][:, t:t + m, :].rearrange("p t d -> p (t d)"),
                                                        bank[BX[t // 2]][:, 0:m * D], ALU.add),
                    [("up", g), ("xs", g)] + prev("o", g, 2), ("x1", g) if t + 2 >= n else ("x1a", g))
            for t in range(n):
                dve(lambda e, t=t: e.bn_stats(stat[:, t, :], xq[:, t, :]), [("x1", g)], ("stat", g, t))
            for t in range(n):
                dve(lambda e, t=t: e.bn_aggr(mv[:, t, :], stat[:, t, :]), [("stat", g, t)] + prev("xn", g), ("mv", g, t))
            dve(lambda e: e.tensor_scalar(var_eps[:, 0:n], mv[:, 0:n, 1], EPS, None, ALU.add), [("mv", g, n - 1)], ("var_eps", g))
            pool(lambda e: e.tensor_tensor(rs[:, 0:n], var_eps[:, 0:n], minus_half[:, 0:n], ALU.pow), [("var_eps", g), "minus_half"] + prev("xn", g), ("rs", g))
            for t in range(n):
                dve(lambda e, t=t: e.tensor_scalar(xn[:, t, :], xq[:, t, :], mv[:, t, 0:1], rs[:, t:t + 1], ALU.subtract, ALU.mult),
                    [("rs", g)] + prev("y_ps", g), ("xn", g) if t == n - 1 else None)

        def light_y_t(g):
            n = nt[g]
            for k in range(K):
                for t in range(n):
                    pe(lambda e, k=k, t=t: e.transpose(bank[BX[k]][:, t * P:(t + 1) * P], xn[:, t, k * P:(k + 1) * P], ident[:]),
                       [("xn", g)], ("y_ps", g) if (k, t) == (K - 1, n - 1) else None)
            for k in range(K):
                act(lambda e, k=k: e.activation(yt[:, k, 0:n * P], bank[BX[k]][:, 0:n * P], ACT.Copy), [("y_ps", g)], ("yt", g) if k == K - 1 else None)

        def light_gate(g):
            n = nt[g]
            gp = bank[BS][:, 0:n * E_]
            for t in range(n):
                at = gp[:, t * E_:(t + 1) * E_]
                for k in range(K):
                    pe(lambda e, k=k, t=t, at=at: e.matmul(at, yt[:, k, t * P:(t + 1) * P], wg[:, k, :], start=k == 0, stop=k == K - 1),
                       [("yt", g), ("pre", g)], ("gate_ps", g) if (t, k) == (n - 1, K - 1) else None)
            g3 = gp.rearrange("p (t c) -> p t c", c=E_)
            dve(lambda e: e.tensor_tensor(sc[:, 0:n, :], g3, b3r(bg, n, E_), ALU.add), [("gate_ps", g)], ("logits", g))
            dve(lambda e: e.tensor_reduce(gm[:, 0:n], sc[:, 0:n, :], AX.X, ALU.max), [("logits", g)], ("gm", g))
            dve(lambda e: e.tensor_tensor(lg[:, 0:n, :], sc[:, 0:n, :], b3d(gm[:, 0:n], n, E_), ALU.subtract), [("gm", g)], ("lg", g))
            act(lambda e: e.activation(ge[:, 0:n, :], lg[:, 0:n, :], ACT.Exp), [("lg", g)], ("ge", g))

        def light_top2(g):
            n = nt[g]
            last = [("ge", g)]
            at = [0]

            def link(emit):
                at[0] += 1
                dve(emit, [last[0]], ("top", g, at[0]))
                last[0] = ("top", g, at[0])
            v = lambda a: a[:, 0:n, :]
            c = lambda a: b3d(a[:, 0:n], n, E_)
            link(lambda e: e.tensor_reduce(m1[:, 0:n], v(ge), AX.X, ALU.add))
            link(lambda e: e.reciprocal(m2[:, 0:n], m1[:, 0:n]))
            link(lambda e: e.tensor_tensor(v(ge), v(ge), c(m2), ALU.mult))

            def pick(m, sel):
                link(lambda e: e.tensor_reduce(m[:, 0:n], v(ge), AX.X, ALU.max))
                link(lambda e: e.tensor_tensor(v(sc), v(ge), c(m), ALU.is_equal))
                link(lambda e: e.tensor_tensor(v(sc), v(sc), b3r(first_rank[:], n, E_), ALU.mult))
                link(lambda e: e.tensor_reduce(mt[:, 0:n], v(sc), AX.X, ALU.max))
                link(lambda e: e.tensor_tensor(v(sel), v(sc), c(mt), ALU.is_equal))
            pick(m1, sel1)
            link(lambda e: e.scalar_tensor_tensor(v(ge), v(sel1), -2.0, v(ge), ALU.mult, ALU.add))
            pick(m2, sel2)
            link(lambda e: e.tensor_tensor(mt[:, 0:n], m2[:, 0:n], m1[:, 0:n], ALU.subtract))
            act(lambda e: e.activation(wb[:, 0:n], mt[:, 0:n], ACT.Exp), [last[0]], ("e2", g))
            last[0] = ("e2", g)
            link(lambda e: e.tensor_scalar(mt[:, 0:n], wb[:, 0:n], 1.0, None, ALU.add))
            link(lambda e: e.reciprocal(wa[:, 0:n], mt[:, 0:n]))
            link(lambda e: e.tensor_tensor(wb[:, 0:n], wb[:, 0:n], wa[:, 0:n], ALU.mult))
            link(lambda e: e.tensor_tensor(v(sel1), v(sel1), c(wa), ALU.mult))
            link(lambda e: e.tensor_tensor(v(sel2), v(sel2), c(wb), ALU.mult))
            dve(lambda e: e.tensor_tensor(w5[:, 0:n, 0:E_], v(sel1), v(sel2), ALU.add), [last[0]], ("w5", g))
            for t in range(n):
                pool(lambda e, t=t: e.tensor_copy(w_wide[:, t, :, :].rearrange("p q (e j) -> p (q e) j", j=H2), b3d(w5[:, t, 0:E_], E_, H2)),
                     [("w5", g)] + prev("spread1", g), ("w_wide", g) if t == n - 1 else None)

        uses = [0]

        def hidden(g, name, out_sb, parts, bias, needs):
            w = nt[g] * P
            u = uses[0]
            uses[0] += 1
            b = bank[BH[u % 2]]
            for i, (po, pn, lhs, rhs, first, final) in enumerate(parts):
                pe(lambda e, po=po, pn=pn, lhs=lhs, rhs=rhs, first=first, final=final: e.matmul(b[po:po + pn, 0:w], lhs, rhs, start=first, stop=final),
                   needs + ([("hid", u - 2)] if u >= 2 else []), ("hid_ps", u) if i == len(parts) - 1 else None)
            act(lambda e: e.activation(out_sb, b[:, 0:w], ACT.Relu, bias=bias), [("hid_ps", u)], ("hid", u))
            steps.value_of[(name, g)] = steps.value_of[("hid", u)]

        def shared1(g, m):
            w = nt[g] * P
            hidden(g, f"h1_{m}", h1[:, m, 0:w], [(0, P, w1[:, k, m * P:(m + 1) * P], yt[:, k, 0:w], k == 0, k == K - 1) for k in range(K)],
                   b_1[:, m:m + 1], [("yt", g)])

        def shared2(g):
            w = nt[g] * P
            hidden(g, "h2", h2[:, 0:w], [(0, P, w2[:, k, :], h1[:, k, 0:w], k == 0, k == K - 1) for k in range(K)], b_2, [("h1_0", g), ("h1_1", g)])

        def expert1(g, x_):
            w = nt[g] * P
            hidden(g, f"e1_{x_}", e1[:, x_, 0:w], [(0, P, we1[:, x_, k, :], yt[:, k, 0:w], k == 0, k == K - 1) for k in range(K)],
                   b_e1[:, x_:x_ + 1], [("yt", g)])

        def expert2(g, q):
            w = nt[g] * P
            hidden(g, f"e2_{q}", e2r[:, q, 0:w], [(i * H2, H2, we2[:, 2 * q + i, :], e1[:, 2 * q + i, 0:w], True, True) for i in range(2)],
                   b_e2[:, q:q + 1], [(f"e1_{2 * q}", g), (f"e1_{2 * q + 1}", g)])

        def weights_t(g):
            n = nt[g]
            for t in range(n):
                pe(lambda e, t=t: e.transpose(bank[BG][0:E_ + 1, t * P:(t + 1) * P], w5[:, t, :], ident[:]),
                   [("w5", g)], ("w5_ps", g) if t == n - 1 else None)
            act(lambda e: e.activation(w5_t[:, 0:n * P], bank[BG][0:E_ + 1, 0:n * P], ACT.Copy), [("w5_ps", g)], ("w5_t", g))

        def spread(g, q):
            n = nt[g]
            for t in range(n):
                pe(lambda e, t=t: e.transpose(bank[BG][:, t * P:(t + 1) * P], w_wide[:, t, q, :], ident[:]),
                   [("w5_t", g) if q == 0 else ("mul0", g), ("w_wide", g)], (f"spread{q}", g) if t == n - 1 else None)
            dve(lambda e: e.tensor_tensor(e2[:, q, 0:n * P], e2r[:, q, 0:n * P], bank[BG][:, 0:n * P], ALU.mult),
                [(f"spread{q}", g), (f"e2_{q}", g)] + prev("out_ps", g), (f"mul{q}", g))

        def final(g, part):
            n = nt[g]
            if part == 0:
                terms = [(h2, w3, ("h2", g)), (w5_t, b3, ("w5_t", g)), (e2[:, 0, :], we3[:, 0, :], ("mul0", g))]
            else:
                terms = [(e2[:, 1, :], we3[:, 1, :], ("mul1", g))]
            for i, (lhs, rhs, need) in enumerate(terms):
                for t in range(n):
                    pe(lambda e, t=t, i=i, lhs=lhs, rhs=rhs: e.matmul(half(BO, t), lhs[:, t * P:(t + 1) * P], rhs, start=part == 0 and i == 0 and t % 2 == 0,
                                                                      stop=part == 1, skip_group_check=True),
                       [need] + (prev("o", g) if part == 0 else []), ("out_ps", g) if (part, t) == (1, n - 1) else None)

        def finish(g):
            n = nt[g]
            for t in range(0, n, 2):
                m = min(2, n - t)
                dve(lambda e, t=t, m=m: e.tensor_tensor(o[g % 2][:, t:t + m, :].rearrange("p t d -> p (t d)"), x1[g % 2][:, t:t + m, :].rearrange("p t d -> p (t d)"),
                                                        bank[BO[t // 2]][:, 0:m * D], ALU.add),
                    [("out_ps", g)] + prev("stored", g, 2), ("o", g) if t + 2 >= n else None)
            full = sum(r == P for r in rows[g])
            r0 = g * TN * P
            if full:
                sp(lambda e: e.dma_start(out[r0:r0 + full * P, :].rearrange("(t p) d -> p t d", p=P), o[g % 2][:, 0:full, :]),
                   [("o", g)], ("stored_full", g), s_out[g % 2])
            if full < n:
                sp(lambda e: e.dma_start(out[r0 + full * P:N, :], o[g % 2][0:rows[g][-1], full, :]), [("o", g)], ("stored_part", g), s_out[g % 2])
            steps.value_of[("stored", g)] = steps.value_of[("stored_part" if full < n else "stored_full", g)]

        load_xs(0)
        light_mean(0)
        for i in range(NG + 1):
            heavy, light = i - 1 if i else None, i if i < NG else None
            after = i + 1 if i + 1 < NG else None
            both = [
                (heavy, lambda g: shared1(g, 0)), (heavy, lambda g: shared1(g, 1)), (light, light_mean_t),
                (heavy, lambda g: expert1(g, 0)), (light, light_fuse), (heavy, lambda g: expert1(g, 1)),
                (heavy, shared2), (light, light_up), (heavy, weights_t), (heavy, lambda g: expert2(g, 0)),
                (heavy, lambda g: expert1(g, 2)), (heavy, lambda g: spread(g, 0)), (heavy, lambda g: expert1(g, 3)),
                (heavy, lambda g: final(g, 0)), (light, light_y_t), (heavy, lambda g: expert2(g, 1)),
                (heavy, lambda g: spread(g, 1)), (after, light_mean), (light, light_gate), (heavy, lambda g: final(g, 1)),
                (light, light_top2), (heavy, finish),
            ]
            if i + 1 < NG:
                load_xs(i + 1)
            for g, step in both:
                if g is not None:
                    step(g)

        def wait_outputs(e):
            for g in range(max(0, NG - 2), NG):
                at, value = steps.value_of[("stored", g)]
                e.wait_ge(at, value)

        with nc.Block() as block:
            @block.sync
            def _(e):
                steps.emit("sp", e)
                wait_outputs(e)

            @block.tensor
            def _(e):
                steps.emit("pe", e)

            @block.vector
            def _(e):
                steps.emit("dve", e)

            @block.scalar
            def _(e):
                steps.emit("act", e)

            @block.gpsimd
            def _(e):
                steps.emit("pool", e)


def kernel(**inputs):
    import concourse.bacc as bacc
    from concourse.bass_utils import run_bass_kernel_spmd

    a = {k: np.asarray(v) for k, v in inputs.items()}
    n, d = a["x"].shape
    edges, ed = a["edge_attr_32"].shape
    node_tiles = -(-n // P)
    tg = 5
    tiles = -(-edges // (P * tg)) * tg
    assert n < node_tiles * P
    src = np.full((tiles * P,), node_tiles * P - 1, np.int32)
    src[:edges] = a["src"]
    attr = np.zeros((ed, tiles * P), np.float32)
    attr[:, :edges] = a["edge_attr_32"].T
    g, f = "L0_gnn_", "L0_ffn_"

    def by_partition(w):
        return w.reshape(-1, P, w.shape[-1]).transpose(1, 0, 2)

    ew1, ew2, ew3 = a[f + "eW1"], a[f + "eW2"], a[f + "eW3"]
    e, _, h1 = ew1.shape
    h2 = ew2.shape[2]
    parts = {
        "wd": by_partition(a[g + "W_down"].T), "wt": np.vstack([a[g + "W_time"].T, a[g + "b_time"][None]]),
        "wf_node": a[g + "W_fusion"].T[:len(a[g + "b_down"])], "wf_time": a[g + "W_fusion"].T[len(a[g + "b_down"]):],
        "wu": np.vstack([a[g + "W_up"].T, a[g + "b_up"][None]]),
        "w1": by_partition(a[f + "sW1"]), "w2": by_partition(a[f + "sW2"]), "w3": a[f + "sW3"],
        "we1": ew1.reshape(e, -1, P, h1).transpose(2, 0, 1, 3), "we2": ew2.transpose(1, 0, 2),
        "we3": ew3.reshape(e // 2, 2 * h2, -1).transpose(1, 0, 2), "b3": np.vstack([a[f + "eb3"], a[f + "sb3"][None]]),
        "wg": by_partition(a[f + "gW"]), "bg": np.broadcast_to(a[f + "gb"], (P, e)),
        "b_d": a[g + "b_down"][:, None], "b_f": a[g + "b_fusion"][:, None],
        "b_1": a[f + "sb1"].reshape(-1, P).T, "b_2": a[f + "sb2"][:, None],
        "b_e1": a[f + "eb1"].T, "b_e2": a[f + "eb2"].reshape(e // 2, -1).T,
    }
    dims = (d, len(a[g + "b_down"]), ed, a[f + "sW1"].shape[1], a[f + "sW2"].shape[1], e, h1, h2, ew3.shape[2])
    columns = weight_columns(*dims)
    weights = np.zeros((P, sum(int(np.prod(shape)) for _, shape in columns.values())), np.float32)
    at = 0
    for name, (used, shape) in columns.items():
        free = int(np.prod(shape))
        weights[:used, at:at + free] = parts[name].reshape(used, free)
        at += free
    given = [("x", a["x"]), ("src_t", src.reshape(tiles, P).T), ("attr_t", attr), ("weights", weights)]

    nc = bacc.Bacc("TRN2", target_bir_lowering=False, num_devices=1)
    arrays, args = {}, []
    for name, v in given:
        v = np.ascontiguousarray(v)
        arrays[f"in_{name}"] = v
        args.append(nc.dram_tensor(f"in_{name}", v.shape, mybir.dt.from_np(v.dtype), kind="ExternalInput").ap())
    args.append(nc.dram_tensor("out_rows", (n, d), mybir.dt.float32, kind="ExternalOutput").ap())
    gnn_ffn(nc, *args[:-1], dims, args[-1])
    return run_bass_kernel_spmd(nc, [arrays], core_ids=[0]).results[0]["out_rows"]
```

```python
from contextlib import ExitStack

import concourse.bass as bass
import numpy as np
from concourse import mybir

P = 128


class Steps:

    def __init__(self):
        self.value_of = {}
        self.counts = {}
        self.queues = {}

    def engine(self, name, own_sem):
        queue = []
        self.queues[name] = queue

        def do(emit, needs=(), mark=None, sem=None):
            at = own_sem if sem is None else sem
            by = 1 if sem is None else 16
            signalled = mark is not None
            if signalled:
                self.counts[at] = self.counts.get(at, 0) + by
                assert mark not in self.value_of, mark
                self.value_of[mark] = (at, self.counts[at])
            queue.append((needs, emit, at if signalled else None, by))

        return do

    def emit(self, name, engine):
        seen = {}
        for needs, emit, sem, by in self.queues[name]:
            for need in needs:
                at, value = self.value_of[need]
                if seen.get(at, 0) < value:
                    engine.wait_ge(at, value)
                    seen[at] = value
            ins = emit(engine)
            if sem is not None:
                ins.then_inc(sem, by)


def weight_columns(d, a, ed, sh1, sh2, e, h1, h2, out):
    k = d // P
    return {
        "wd": (P, (k, a)), "wt": (ed + 1, (a,)), "wf_node": (a, (a,)), "wf_time": (a, (a,)), "wu": (a + 1, (d,)),
        "w1": (P, (k, sh1)), "we1": (P, (e, k, h1)), "w2": (P, (k, sh2)), "w3": (P, (out,)), "we2": (P, (e, h2)),
        "we3": (P, (e // 2, out)), "b3": (9 * (e + 1), (out,)), "b3_part": (9 * (e + 1), (3,)), "spread": (9 * (e + 1), (e // 2, P)), "wg": (P, (k, e)), "bg": (P, (e,)),
        "b_d": (a, (1,)), "b_f": (a, (1,)), "b_1": (P, (k,)), "b_2": (P, (1,)), "b_e1": (P, (e,)), "b_e2": (P, (e // 2,)),
    }


def gnn_ffn(nc, x, src_t, attr_t, weights, dims, out):
    f32r = mybir.dt.float32r
    f32, bf16, i32 = mybir.dt.float32, mybir.dt.bfloat16, mybir.dt.int32
    ALU, ACT, AX = mybir.AluOpType, mybir.ActivationFunctionType, mybir.AxisListType

    N, D = x.shape
    ET = src_t.shape[1]
    D, A, ED, SH1, SH2, E_, H1, H2, OUT = dims
    NT = -(-N // P)
    TG = 5
    EG = ET // TG
    assert TG * NT <= 512 and ET % TG == 0
    LG = 3
    NL = -(-EG // LG)
    R = 2
    CH = R * P
    SH = CH.bit_length() - 1
    CL = 8
    SHARES = (42, 35, 23)
    cuts = [0]
    for share in SHARES[:-1]:
        cuts.append(cuts[-1] + max(LG, EG * share // 100 // LG * LG))
    cuts.append(EG)
    parts = [(cuts[k], cuts[k + 1]) for k in range(len(SHARES))]
    part_of = [k for k, (g0, g1) in enumerate(parts) for _ in range(g0, g1)]
    loads = [-(-((g1 - g0) * TG * P // CH + NT) // CL) for g0, g1 in parts]
    n_ch = [n * CL for n in loads]
    offs_at = [sum(n_ch[:k]) for k in range(len(parts))]
    PT = max(g1 - g0 for g0, g1 in parts) * TG
    ONE, MID, LOW, LO, ROW = A, A + 1, 2 * A + 1, 3 * A + 1, 3 * A + 2
    SW = A + 1
    Z = 64
    TN = 4
    NG = -(-NT // TN)
    K = D // P
    assert (A, D, H1, H2, E_, SH1, SH2, OUT) == (64, 256, 128, 64, 4, 256, 128, 256)
    EPS = 1e-5
    nt = [min(TN, NT - TN * g) for g in range(NG)]
    rows = [[min(P, N - (TN * g + t) * P) for t in range(nt[g])] for g in range(NG)]

    tables = [nc.dram_tensor(f"table{k}", (n * CH, ROW), bf16, kind="Internal").ap() for k, n in enumerate(n_ch)]
    fused_dram = nc.dram_tensor("fused_node", (NG * A, TN * P), f32, kind="Internal").ap()
    x_ln = nc.dram_tensor("x_ln", (NG * P, TN * D), f32, kind="Internal").ap()

    with ExitStack() as ctx:
        def sb(name, shape, dt):
            return ctx.enter_context(nc.sbuf_tensor(name, shape, dt))

        def sem(name):
            return ctx.enter_context(nc.semaphore(name))

        s_pe, s_dve, s_act, s_pool = sem("s_pe"), sem("s_dve"), sem("s_act"), sem("s_pool")
        s_w, s_src, s_zero_ends = sem("s_w"), sem("s_src"), sem("s_zero_ends")
        s_zero_tail = [sem(f"s_zero_tail{k}") for k in range(len(parts))]
        NA, NP, NTB = 2, 6, 3
        s_attr = [sem(f"s_attr{i}") for i in range(NA)]
        s_scatter = [sem(f"s_scatter{i}") for i in range(NP)]
        s_fused = [sem(f"s_fused{i}") for i in range(2)]
        s_fused_in = [sem(f"s_fused_in{i}") for i in range(2)]
        s_table = [sem(f"s_table{i}") for i in range(NTB)]
        s_x = [sem(f"s_x{i}") for i in range(2)]
        s_xln = [sem(f"s_xln{i}") for i in range(2)]
        s_xln_in = [sem(f"s_xln_in{i}") for i in range(2)]
        s_out = [sem(f"s_out{i}") for i in range(2)]

        w_all = sb("w_all", list(weights.shape), f32)
        views, at, starts = {}, 0, {}
        for name, (used, shape) in weight_columns(*dims).items():
            free = int(np.prod(shape))
            v = w_all[0:used, at:at + free]
            starts[name] = at
            at += free
            if len(shape) > 1:
                names = "abc"[:len(shape)]
                v = v.rearrange(f"p ({' '.join(names)}) -> p {' '.join(names)}", **dict(zip(names[1:], shape[1:])))
            views[name] = v
        wd, wf_node, wf_time = views["wd"], views["wf_node"], views["wf_time"]
        wt = views["wt"]
        wu = views["wu"]
        w2, w3, wg, bg = views["w2"], views["w3"], views["wg"], views["bg"]
        we2 = views["we2"]
        w1_at, w1_end = starts["w1"], starts["we1"] + E_ * K * H1
        w1_halves = [sb(f"w1_{half}", [P, w1_end - w1_at], f32r) for half in ("high", "low")]
        w1 = [w[:, 0:K * SH1].rearrange("p (k m) -> p k m", k=K) for w in w1_halves]
        we1 = [w[:, K * SH1:].rearrange("p (e k m) -> p e k m", e=E_, k=K) for w in w1_halves]
        yt_halves = [sb(f"yt_{half}", [P, K, TN * P], f32r) for half in ("high", "low")]
        HIGH_BITS = -(1 << 12)
        we3 = views["we3"]
        b3, b3_part = views["b3"], views["b3_part"]
        S = 9 * (E_ + 1)
        b_d, b_f, b_1, b_2 = views["b_d"], views["b_f"], views["b_1"], views["b_2"]
        b_e1, b_e2 = views["b_e1"], views["b_e2"]
        b3_bf = sb("b3_bf", [S, OUT], bf16)
        spread_bf = sb("spread_bf", [S, E_ // 2, P], bf16)
        iota_row = sb("iota_row", [P, P], f32)
        iota_col = sb("iota_col", [P, 1], f32)
        iota_bf = sb("iota_bf", [P, P], bf16)
        iota_wide = sb("iota_wide", [P, P, CL * R], bf16)
        ident = sb("ident", [P, P], f32)
        before = sb("before", [P, P], bf16)
        notbefore = sb("notbefore", [P, P], bf16)
        ones_bf = sb("ones_bf", [P, P], bf16)
        ones = sb("ones", [P, P], f32)
        eps_col = sb("eps_col", [P, 1], f32)
        first_rank = sb("first_rank", [P, E_], f32)
        sums_all = sb("sums", [P, max(NT * SW, Z * ROW // 2)], f32)
        sums = sums_all[:, 0:NT * SW]
        offs = sb("offs", [1, sum(n_ch)], i32)

        ARENA = 34650
        arena = sb("arena", [P, ARENA], f32)
        top = [0]

        def carve(shape, dt, partitions=P):
            free = int(np.prod(shape))
            words = free if dt != bf16 else (free + 1) // 2
            a = arena[0:partitions, top[0]:top[0] + words]
            top[0] += words
            assert top[0] <= ARENA, top[0]
            if dt != f32:
                a = a.bitcast(dt)[:, 0:free]
            if len(shape) == 1:
                return a
            names = "abcd"[:len(shape)]
            return a.rearrange(f"p ({' '.join(names)}) -> p {' '.join(names)}",
                               **dict(zip(names[1:], shape[1:])))

        b3_high = carve([OUT], bf16, S)
        b3_mid = carve([OUT], bf16, S)
        b3_rest = carve([OUT], f32, S)
        b3_sum = carve([OUT], f32, S)
        w1_top = carve([(K * SH1 + E_ * K * H1) // 4], f32)
        hi = carve([ET], bf16)
        lo = carve([ET], bf16)
        thr = carve([NT], f32)
        ge_count = carve([NT + 1], f32)
        tot = carve([NT + 1], f32)
        n_i = carve([NT], i32)
        c_i = carve([NT], i32)
        n_chunks = carve([NT], f32)
        end_chunk = carve([NT], f32)
        first_chunk = carve([NT], f32)
        last_chunk = carve([NT], f32)
        zeros_row = carve([NT], f32)
        base = [carve([NT], f32) for _ in parts]
        chunk_col = carve([2], f32)
        zero_idx = carve([CH // Z], i32)
        iota_chunk = carve([max(n_ch)], f32)
        started = carve([max(n_ch)], bf16)
        attr = [carve([LG * TG * P], f32, ED + 1) for _ in range(NA)]
        pay = [carve([TG, ROW], bf16) for _ in range(NP)]
        pos = [carve([TG], i32) for _ in range(NP)]
        onehot = [carve([TG, NT], bf16) for _ in range(2)]
        picked = carve([TG, NT], f32)
        rest = [carve([TG, A], f32) for _ in range(2)]
        tab = [carve([CL, R, ROW], bf16) for _ in range(NTB)]
        hot = [carve([P, CL * R], bf16) for _ in range(2)]
        tab_lo = [carve([CL, R], bf16) for _ in range(2)]
        sums_odd = carve([NT * SW], f32)
        junk_v = [carve([PT], bf16) for _ in range(2)]
        junk_a = [carve([PT], bf16) for _ in range(2)]
        shared_from = top[0]
        src_i = carve([ET], i32)
        hi_i = carve([ET], i32)
        lo_i = carve([ET], i32)
        used_0 = top[0]
        top[0] = shared_from
        xa = [carve([TN, D], f32) for _ in range(2)]
        xn_a = carve([TN, D], f32)
        xs_a = carve([TN, D], f32)
        xt_a = carve([K, TN * P], f32)
        nf_a = carve([TN * P], f32, A)
        fused_a = [carve([TN * P], f32, A) for _ in range(2)]
        stat_a = carve([TN, 6], f32)
        mv_a = carve([TN, 2], f32)
        sd_a = carve([TN], f32)
        rs_a = carve([TN], f32)
        used_1 = max(top[0], used_0)
        top[0] = 0
        time_sum = carve([TN, SW], f32)
        cnt = carve([TN], f32)
        rcnt = carve([TN], f32)
        ntf = carve([TN, A], f32)
        ntf_t = carve([TN * P], f32, A)
        fused_in = [carve([TN * P], f32, A) for _ in range(2)]
        pre = carve([TN * P], f32, A)
        fused = carve([TN * P], f32, A + 1)
        xs = [carve([TN, D], f32) for _ in range(2)]
        x1 = [carve([TN, D], f32) for _ in range(2)]
        xn = carve([TN, D], f32)
        stat = carve([TN, 6], f32)
        mv = carve([TN, 2], f32)
        var_eps = carve([TN], f32)
        minus_half = carve([TN], f32)
        rs = carve([TN], f32)
        yt = carve([K, TN * P], f32)
        yt_top = carve([K, TN * P], f32)
        h1 = carve([K, TN * P], f32)
        h2 = carve([TN * P], f32)
        e1 = carve([E_, TN * P], f32)
        e2r = carve([2, TN * P], f32)
        e2 = carve([2, TN * P], f32)
        lg = carve([TN, E_], f32)
        gm = carve([TN], f32)
        ge = carve([TN, E_], f32)
        sel1 = carve([TN, E_], f32)
        sel2 = carve([TN, E_], f32)
        sc = carve([TN, E_], f32)
        m1 = carve([TN], f32)
        m2 = carve([TN], f32)
        mt = carve([TN], f32)
        wa = carve([TN], f32)
        wb = carve([TN], f32)
        w4 = carve([TN, E_], f32)
        w4_high = carve([TN, E_], bf16)
        w4_rest = carve([TN, E_], f32)
        w4_mid = carve([TN, E_], bf16)
        w5 = carve([TN, 3, 3, E_ + 1], f32)
        w5_t = carve([TN * P], bf16, S)
        o = [carve([TN, D], f32) for _ in range(2)]
        assert max(used_1, top[0]) <= ARENA, (used_1, top[0])

        bank = [ctx.enter_context(nc.psum_tensor(f"bank{i}", [P, 512], f32)) for i in range(8)]

        steps = Steps()
        sp = steps.engine("sp", None)
        pe = steps.engine("pe", s_pe)
        dve = steps.engine("dve", s_dve)
        act = steps.engine("act", s_act)
        pool = steps.engine("pool", s_pool)

        def b3d(a, n, m):
            return a.unsqueeze(2).to_broadcast([a.shape[0], n, m])

        def b3r(a, n, m):
            return a.unsqueeze(1).to_broadcast([a.shape[0], n, m])

        sp(lambda e: e.dma_start(src_i, src_t), mark="src", sem=s_src)
        sp(lambda e: e.dma_start(w_all[:], weights), mark="weights", sem=s_w)

        def load_attr(n):
            first, m = n * LG, min(LG, EG - n * LG)
            needs = [("feat", (n - NA) * LG + LG - 1)] if n >= NA else [("attr_ones", NA - 1)]
            sp(lambda e: e.dma_start(attr[n % NA][0:ED, 0:m * TG * P],
                                     attr_t[:, first * TG * P:(first + m) * TG * P]),
               needs, ("attr", n), s_attr[n % NA])

        pool(lambda e: e.iota(iota_row[:], pattern=[[1, P]], base=0, channel_multiplier=0,
                              allow_small_or_imprecise_dtypes=True))
        pool(lambda e: e.iota(iota_bf[:], pattern=[[1, P]], base=0, channel_multiplier=0,
                              allow_small_or_imprecise_dtypes=True))
        pool(lambda e: e.iota(iota_col[:], pattern=[[0, 1]], base=0, channel_multiplier=1,
                              allow_small_or_imprecise_dtypes=True))
        pool(lambda e: e.iota(first_rank[:], pattern=[[-1, E_]], base=E_, channel_multiplier=0,
                              allow_small_or_imprecise_dtypes=True))
        pool(lambda e: e.iota(iota_chunk, pattern=[[1, max(n_ch)]], base=0, channel_multiplier=0,
                              allow_small_or_imprecise_dtypes=True), mark="iota")
        dve(lambda e: e.tensor_scalar(thr, iota_row[:, 0:NT], -1.0, 0.5, ALU.mult, ALU.add), ["iota"], "thr")
        dve(lambda e: e.tensor_scalar(hi_i, src_i, 7, None, ALU.arith_shift_right), ["src"], "hi_i")
        dve(lambda e: e.tensor_copy(hi, hi_i), ["hi_i"], "hi")
        pool(lambda e: e.memset(sums_all[:], 0.0), ["iota"], "zeros")
        before_it = "zeros"
        for i, a in enumerate(attr):
            pool(lambda e, a=a: e.memset(a[ED:ED + 1, :], 1.0), [before_it], ("attr_ones", i))
            before_it = ("attr_ones", i)
        pool(lambda e: e.memset(sums_odd, 0.0), [before_it], "sums_odd")
        before_it = "sums_odd"
        dve(lambda e: e.memset(ones_bf[:], 1.0))
        dve(lambda e: e.memset(ones[:], 1.0))
        dve(lambda e: e.memset(eps_col[:], EPS))
        dve(lambda e: e.memset(zeros_row, 0.0))
        dve(lambda e: e.memset(ge_count[:, NT:NT + 1], 0.0))
        for i, q in enumerate(pay):
            pool(lambda e, q=q: e.memset(q[:, :, ONE:ONE + 1], 1.0), [before_it], ("pay_one", i))
            before_it = ("pay_one", i)
        dve(lambda e: e.tensor_copy(iota_wide[:], b3d(iota_bf[:], P, CL * R)))
        dve(lambda e: e.tensor_scalar(before[:], iota_row[:], iota_col[:, 0:1], None, ALU.is_gt))
        dve(lambda e: e.tensor_scalar(notbefore[:], iota_row[:], iota_col[:, 0:1], None, ALU.is_le))
        dve(lambda e: e.tensor_scalar(ident[:], iota_row[:], iota_col[:, 0:1], None, ALU.is_equal), mark="const")

        zsrc = sums_all[:].bitcast(bf16)

        def zero_tail(k):
            g0, g1 = parts[k]
            dmas = []
            for r0 in range((g1 - g0) * TG * P, n_ch[k] * CH, P * Z):
                m = min(P * Z, n_ch[k] * CH - r0)
                q, left = m // Z, m % Z
                for c0, cn, w in ((r0, q, Z), (r0 + q * Z, 1, left)):
                    if cn and w:
                        def zero(c0=c0, cn=cn, w=w):
                            sp(lambda e: e.dma_start(
                                tables[k][c0:c0 + cn * w, :].rearrange("(p r) c -> p (r c)", r=w), zsrc[0:cn, 0:w * ROW]),
                               ["zeros"], ("tail", k, c0), s_zero_tail[k])
                            steps.value_of[("tail", k)] = steps.value_of[("tail", k, c0)]
                        dmas.append(zero)
            return dmas
        for zero in zero_tail(0):
            zero()
        for n in range(min(NA, NL)):
            load_attr(n)


        def tiles_of(k):
            return hi[:, parts[k][0] * TG:parts[k][1] * TG], (parts[k][1] - parts[k][0]) * TG

        def sign_count(k, c):
            h, n = tiles_of(k)
            act(lambda e: e.activation(junk_a[c % 2][:, 0:n], h, ACT.Sign, bias=thr[:, c:c + 1], accum_out=ge_count[:, c:c + 1]),
                ["hi", "thr"] + ([("sign", k, c - 2)] if c > 2 else []) + ([("tot_ps", k - 1)] if k else []), ("sign", k, c))

        def compare_count(k, c, first):
            h, n = tiles_of(k)
            dve(lambda e: e.tensor_scalar(junk_v[c % 2][:, 0:n], h, float(c), None, ALU.is_ge, ALU.add, accum_out=ge_count[:, c:c + 1]),
                ["hi"] + ([("ge", k, c - 2)] if c >= first + 2 else []), ("ge", k, c))

        def sizes(k, split):
            n = tiles_of(k)[1]
            ps = bank[6]
            dve(lambda e: e.memset(ge_count[:, 0:1], float(n)), [("tot_ps", k - 1)] if k else [], ("ge_all", k))
            dve(lambda e: e.tensor_scalar(ge_count[:, 1:split], ge_count[:, 1:split], float(n), 0.5, ALU.add, ALU.mult),
                [("sign", k, split - 1)], ("ge_count", k))
            pe(lambda e: e.matmul(ps[:, 0:NT + 1], ones[:], ge_count, start=True, stop=True),
               [("ge_count", k), "const"] + last_read[6] + ([("ge", k, NT - 1)] if split < NT else []), ("tot_ps", k))
            dve(lambda e: e.tensor_copy(tot, ps[:, 0:NT + 1]), [("tot_ps", k)], ("tot", k))
            dve(lambda e: e.tensor_tensor(n_i, tot[:, 0:NT], tot[:, 1:NT + 1], ALU.subtract), [("tot", k)], ("n_i", k))
            dve(lambda e: e.tensor_scalar(c_i, n_i, SH, None, ALU.arith_shift_right), [("n_i", k)], ("c_i", k))
            dve(lambda e: e.tensor_scalar(n_chunks, c_i, 1.0, None, ALU.add), [("c_i", k)], ("n_chunks", k))
            dve(lambda e: e.tensor_tensor_scan(end_chunk, n_chunks, zeros_row, 0.0, ALU.add, ALU.add), [("n_chunks", k)], ("end_chunk", k))
            dve(lambda e: e.tensor_tensor(first_chunk, end_chunk, n_chunks, ALU.subtract), [("end_chunk", k)], ("first_chunk", k))
            dve(lambda e: e.tensor_scalar(last_chunk, end_chunk, -1.0, None, ALU.add), (), ("last_chunk", k))
            dve(lambda e: e.tensor_scalar(base[k], first_chunk, float(CH), None, ALU.mult), [("first_chunk", k)], ("base", k))
            pe(lambda e: e.matmul(ps[0:NT, 128:129], first_chunk[0:1, :], ones[0:1, 0:1], start=True, stop=True), [("first_chunk", k), ("tot", k)])
            pe(lambda e: e.matmul(ps[0:NT, 129:130], last_chunk[0:1, :], ones[0:1, 0:1], start=True, stop=True), [("last_chunk", k)], ("chunk_ps", k))
            dve(lambda e: e.tensor_copy(chunk_col[0:NT, :], ps[0:NT, 128:130]), [("chunk_ps", k)], ("chunk_col", k))
            last_read[6] = [("chunk_col", k)]
            for r in range(CH // Z):
                dve(lambda e, r=r: e.tensor_scalar(zero_idx[0:NT, r:r + 1], chunk_col[0:NT, 1:2], float(CH // Z), float(r), ALU.mult, ALU.add),
                    [("chunk_col", k)] + ([("ends", k - 1)] if k else []), ("zero_idx", k, r))
            dve(lambda e: e.tensor_scalar(started[0:NT, 0:n_ch[k]], iota_chunk[0:NT, 0:n_ch[k]], chunk_col[0:NT, 0:1], None, ALU.is_ge),
                [("chunk_col", k)], ("started", k))
            for i, c0 in enumerate(range(0, n_ch[k], 512)):
                w = min(512, n_ch[k] - c0)
                b = bank[7 - i % 2][0:1, 0:w]
                pe(lambda e, c0=c0, w=w, b=b: e.matmul(b, ones_bf[0:NT, 0:1], started[0:NT, c0:c0 + w], start=True, stop=True),
                   [("started", k)] + last_read[7 - i % 2], ("offs_ps", k, i))
                dve(lambda e, k=k, c0=c0, w=w, b=b: e.tensor_scalar(offs[0:1, offs_at[k] + c0:offs_at[k] + c0 + w], b, -1.0, float(SW), ALU.add, ALU.mult),
                    [("offs_ps", k, i)], ("offs", k, i))
                last_read[7 - i % 2] = [("offs", k, i)]
            steps.value_of[("sized", k)] = steps.value_of[("offs", k, (n_ch[k] - 1) // 512)]

        last_read = {6: [], 7: []}
        def zero_ends(k):
            zrows = tables[k].rearrange("(n r) c -> n (r c)", r=Z)
            return [lambda r=r: pool(lambda e: e.indirect_dma_start(
                out=zrows, out_offset=bass.IndirectOffsetOnAxis(ap=zero_idx[0:NT, r:r + 1], axis=0),
                in_=zsrc[0:NT, 0:Z * ROW], in_offset=None, bounds_check=n_ch[k] * CH // Z - 1, oob_is_err=False),
                [("zero_idx", k, r), ("tail", k)], ("ends", k) if r == CH // Z - 1 else ("end", k, r), s_zero_ends)
                for r in range(CH // Z)]

        split = 1 + (NT - 1) * 42 // 100
        dve(lambda e: e.tensor_scalar(lo_i, src_i, 127, None, ALU.bitwise_and), (), "lo_i")
        dve(lambda e: e.tensor_copy(lo, lo_i), ["lo_i"], "lo")
        for c in range(1, split):
            sign_count(0, c)
        for c in range(split, NT):
            compare_count(0, c, split)
        sizes(0, split)
        for zero in zero_ends(0):
            zero()

        places = bank[0][:, 0:TG * NT]
        places3 = places.rearrange("p (j b) -> p j b", j=TG)
        def feat_ps(g):
            return bank[1 + g % 2][:, 0:TG * A].rearrange("p (j a) -> p j a", j=TG)

        def free(g):
            return [("scattered", g - NP)] if g >= NP else []

        def bucket_onehot(g):
            dve(lambda e: e.tensor_tensor(onehot[g % 2], b3r(iota_bf[:, 0:NT], TG, NT), b3d(hi[:, g * TG:(g + 1) * TG], TG, NT), ALU.is_equal),
                [("counted", g - 2)] if g >= 2 else ["hi"], ("onehot", g))

        def features(g):
            for j in range(TG):
                t = (g % LG) * TG + j
                pe(lambda e, j=j, t=t: e.matmul(feat_ps(g)[:, j, :], attr[g // LG % NA][:, t * P:(t + 1) * P], wt, start=True, stop=True),
                   [("attr", g // LG), "weights", ("sized", 0)] + ([("rest", g - 2)] if g >= 2 else []), ("feat", g) if j == TG - 1 else None)

        def find_places(g):
            hot_g = onehot[g % 2]
            k = part_of[g]
            if g == parts[k][0]:
                pe(lambda e: e.matmul(places, ones[0:1, :], b3r(base[k][0:1, :], TG, NT), start=True, stop=True, skip_group_check=True),
                   [("base", k)] + ([("picked", g - 1)] if g else []), ("placed", k))
            pe(lambda e: e.matmul(places, before[:], hot_g.rearrange("p j b -> p (j b)"), start=False, stop=True, skip_group_check=True), [("onehot", g), "const"])
            for i in range(TG - 1):
                pe(lambda e, i=i: e.matmul(places3[:, i + 1:TG, :], ones_bf[:], b3r(hot_g[:, i, :], TG - 1 - i, NT), start=False, stop=True, skip_group_check=True),
                   (), ("places", g) if i == TG - 2 else None)
            dve(lambda e: e.tensor_tensor(picked, places3, hot_g, ALU.mult), [("places", g)] + ([("pos", g - 1)] if g else []), ("picked", g))

            def reduce_places(e):
                with nc.allow_low_precision(reason="one whole number below 2^24 and zeros: exact"):
                    return e.tensor_reduce(pos[g % NP], picked, AX.X, ALU.add)
            dve(reduce_places, [("picked", g)] + free(g), ("pos", g))

        def count_group(g):
            hot_g = onehot[g % 2]
            pe(lambda e: e.matmul(places, notbefore[:], hot_g.rearrange("p j b -> p (j b)"), start=False, stop=True, skip_group_check=True), [("picked", g)])
            for i in range(1, TG):
                pe(lambda e, i=i: e.matmul(places3[:, 0:i, :], ones_bf[:], b3r(hot_g[:, i, :], i, NT), start=False, stop=True, skip_group_check=True),
                   (), ("counted", g) if i == TG - 1 else None)

        def part_high(g):
            q = pay[g % NP]
            act(lambda e: e.activation(q[:, :, 0:A], feat_ps(g), ACT.Relu), [("feat", g)] + free(g), ("high", g))
            act(lambda e: e.activation(q[:, :, LO], lo[:, g * TG:(g + 1) * TG], ACT.Copy), ["lo"], ("lo", g))
            dve(lambda e: e.scalar_tensor_tensor(rest[g % 2], feat_ps(g), 0.0, q[:, :, 0:A], ALU.max, ALU.subtract),
                [("high", g)] + ([("low", g - 2)] if g >= 2 else []), ("rest", g))

        def part_mid(g):
            act(lambda e: e.activation(pay[g % NP][:, :, MID:MID + A], rest[g % 2], ACT.Copy), [("rest", g)], ("mid", g))

        def part_low(g):
            q = pay[g % NP]
            dve(lambda e: e.tensor_tensor(q[:, :, LOW:LOW + A], rest[g % 2], q[:, :, MID:MID + A], ALU.subtract),
                [("mid", g)], ("low", g))

        def scatter(g):
            q = g % NP
            k = part_of[g]
            for j in range(TG):
                pool(lambda e, j=j: e.indirect_dma_start(
                    out=tables[k], out_offset=bass.IndirectOffsetOnAxis(ap=pos[q][:, j:j + 1], axis=0),
                    in_=pay[q][:, j, :], in_offset=None, bounds_check=n_ch[k] * CH - 1, oob_is_err=False),
                     [("low", g), ("pos", g), ("lo", g), ("ends", k), ("pay_one", NP - 1)],
                     ("scattered", g) if j == TG - 1 else ("scattering", g, j), s_scatter[q])

        edge_stages = [(2, count_group), (0, bucket_onehot), (1, find_places), (0, features), (3, part_low), (1, part_high),
                       (2, part_mid), (3, scatter)]
        BEHIND = max(lag for lag, _ in edge_stages)

        def node_first(a):
            n, w = nt[a], nt[a] * P
            xg, xb = xa[a % 2], x[a * TN * P:min((a + 1) * TN * P, N), :]

            def load():
                full = sum(r == P for r in rows[a])
                needs = [("xn_a", a - 2), ("xs_a", a - 2)] if a >= 2 else ["lo"]
                if full:
                    sp(lambda e: e.dma_start(xg[:, 0:full, :], xb[0:full * P, :].rearrange("(t p) d -> p t d", p=P)), needs, ("x_full", a), s_x[a % 2])
                if full < n:
                    sp(lambda e: e.dma_start(xg[0:rows[a][-1], full, :], xb[full * P:, :]), needs, ("x_part", a), s_x[a % 2])
                steps.value_of[("x", a)] = steps.value_of[("x_part" if full < n else "x_full", a)]

            def stats():
                for t in range(n):
                    dve(lambda e, t=t: e.bn_stats(stat_a[:, t, :], xg[:, t, :]), [("x", a)], ("stat_a", a, t))
                for t in range(n):
                    dve(lambda e, t=t: e.bn_aggr(mv_a[:, t, :], stat_a[:, t, :]), [("stat_a", a, t)] + ([("xn_a", a - 1)] if a else []), ("mv_a", a, t))

            def root():
                act(lambda e: e.activation(sd_a[:, 0:n], mv_a[:, 0:n, 1], ACT.Sqrt, bias=eps_col[:]), [("mv_a", a, n - 1)], ("sd_a", a))

            def normed():
                dve(lambda e: e.reciprocal(rs_a[:, 0:n], sd_a[:, 0:n]), [("sd_a", a)], ("rs_a", a))
                for t in range(n):
                    dve(lambda e, t=t: e.tensor_scalar(xn_a[:, t, :], xg[:, t, :], mv_a[:, t, 0:1], rs_a[:, t:t + 1], ALU.subtract, ALU.mult),
                        [("rs_a", a)] + ([("xt_ps", a - 1), ("xs_a", a - 1)] if a else []), ("xn_a", a) if t == n - 1 else None)
                dve(lambda e: e.tensor_tensor(xs_a[:, 0:n, :], xg[:, 0:n, :], xn_a[:, 0:n, :], ALU.add),
                    [("xn_a", a)] + ([("x_ln", a - 1)] if a else []), ("xs_a", a))
                sp(lambda e: e.dma_start(x_ln[a * P:(a + 1) * P, 0:n * D], xs_a[:, 0:n, :].rearrange("p t d -> p (t d)")),
                   [("xs_a", a)], ("x_ln", a), s_xln[a % 2])

            def transposes():
                for k in range(K):
                    for t in range(n):
                        pe(lambda e, k=k, t=t: e.transpose(bank[3 + k][:, t * P:(t + 1) * P], xn_a[:, t, k * P:(k + 1) * P], ident[:]),
                           [("xn_a", a)] + ([("xt_a", a - 1)] if a else []), ("xt_ps", a) if (k, t) == (K - 1, n - 1) else None)

            def evacuate():
                for k in range(K):
                    act(lambda e, k=k: e.activation(xt_a[:, k, 0:w], bank[3 + k][:, 0:w], ACT.Copy),
                        [("xt_ps", a)], ("xt_a", a) if k == K - 1 else None)

            def down():
                for k in range(K):
                    pe(lambda e, k=k: e.matmul(bank[5][0:A, 0:w], wd[:, k, :], xt_a[:, k, 0:w], start=k == 0, stop=k == K - 1),
                       [("xt_a", a)] + ([("fused_a", a - 1)] if a else []), ("down", a) if k == K - 1 else None)

            def down_relu():
                act(lambda e: e.activation(nf_a[:, 0:w], bank[5][0:A, 0:w], ACT.Relu, bias=b_d), [("down", a)], ("nf_a", a))

            def fuse():
                pe(lambda e: e.matmul(bank[5][0:A, 0:w], wf_node, nf_a[:, 0:w], start=True, stop=True), [("nf_a", a)], ("fuse", a))

            def keep():
                act(lambda e: e.activation(fused_a[a % 2][:, 0:w], bank[5][0:A, 0:w], ACT.Identity, bias=b_f),
                    [("fuse", a)] + ([("fused_kept", a - 2)] if a >= 2 else []), ("fused_a", a))

            def store():
                sp(lambda e: e.dma_start(fused_dram[a * A:(a + 1) * A, 0:w], fused_a[a % 2][:, 0:w]), [("fused_a", a)], ("fused_kept", a), s_fused[a % 2])

            return [load, lambda: None, stats, root, normed, transposes, evacuate, down, down_relu, fuse, keep, store]

        period = max(EG // (NG + 1), 1)
        at_group = {}
        for a in range(NG):
            for k, step in enumerate(node_first(a)):
                at_group.setdefault(a * max(period, 11) + k, []).append(step)
        room = max(1, parts[0][1] - 2 * NP - 4 - 4 * (len(parts) - 1) * (CH // Z))
        per = -(-(NT - 1) * (len(parts) - 1) // room)
        at = NP
        for k in range(1, len(parts)):
            for i, zero in enumerate(zero_tail(k)):
                at_group.setdefault(at + 3 * i, []).append(zero)
            for c in range(1, NT, per):
                at_group.setdefault(at, []).append(lambda k=k, c=c: [sign_count(k, x_) for x_ in range(c, min(c + per, NT))])
                at += 1
            at_group.setdefault(at, []).append(lambda k=k: sizes(k, NT))
            for i, zero in enumerate(zero_ends(k)):
                at += 4
                at_group.setdefault(at, []).append(zero)
        all_zeroed = [("ends", len(parts) - 1), ("pay_one", NP - 1)]

        def split_b3():
            dve(lambda e: e.tensor_copy(spread_bf[:], views["spread"]), ["weights"])
            dve(lambda e: e.tensor_copy(b3_high, b3), (), "b3_high")
            dve(lambda e: e.tensor_tensor(b3_rest, b3, b3_high, ALU.subtract), ["b3_high"], "b3_rest")
            dve(lambda e: e.tensor_copy(b3_mid, b3_rest), ["b3_rest"], "b3_mid")
            dve(lambda e: e.tensor_tensor(b3_rest, b3_rest, b3_mid, ALU.subtract), ["b3_mid"], "b3_low")
            dve(lambda e: e.tensor_scalar(b3_sum, b3_high, b3_part[:, 0:1], None, ALU.mult), ["b3_high"], "b3_sum1")
            dve(lambda e: e.scalar_tensor_tensor(b3_sum, b3_mid, b3_part[:, 1:2], b3_sum, ALU.mult, ALU.add), ["b3_sum1", "b3_mid"], "b3_sum2")
            dve(lambda e: e.scalar_tensor_tensor(b3_bf[:], b3_rest, b3_part[:, 2:3], b3_sum, ALU.mult, ALU.add), ["b3_sum2", "b3_low"], "b3_bf")
        at_group.setdefault(NP, []).append(split_b3)

        def split_w1(c):
            n = (w1_end - w1_at) // 4
            at, w = c * n, w_all[:, w1_at + c * n:w1_at + (c + 1) * n]
            dve(lambda e: e.tensor_scalar(w1_top.bitcast(i32), w.bitcast(i32), HIGH_BITS, None, ALU.bitwise_and),
                [("w1_low", c - 1)] if c else ["weights"], ("w1_top", c))
            dve(lambda e: e.tensor_copy(w1_halves[0][:, at:at + n], w1_top), [("w1_top", c)], ("w1_high", c))
            dve(lambda e: e.tensor_tensor(w1_halves[1][:, at:at + n], w, w1_top, ALU.subtract), (), ("w1_low", c))
        for c in range(4):
            at_group.setdefault(NP + 2 + 2 * c, []).append(lambda c=c: split_w1(c))

        regs = []
        hots = [0]

        def sum_steps(k):
            t0 = sum(loads[:k])
            banks = [6, 7] if k < len(parts) - 1 else [3, 4, 5, 6, 7]
            done = [("scattered", g) for g in range(max(0, parts[k][1] - NP), parts[k][1])]

            def load(n):
                t = t0 + n
                sp(lambda e: e.dma_start(tab[t % NTB], tables[k][n * CL * CH:(n + 1) * CL * CH, :].rearrange("(c p r) w -> p c r w", p=P, r=R)),
                   ([("sum_ps", t - NTB)] if t >= NTB else []) + (done if n == 0 else []), ("tab", t), s_table[t % NTB])

            def make_hot(n):
                t = t0 + n
                two = t % 2
                dve(lambda e: e.tensor_copy(tab_lo[two], tab[t % NTB][:, :, :, LO]), [("tab", t)] + ([("hot", t - 2)] if t >= 2 else []), ("tab_lo", t))
                dve(lambda e: e.tensor_tensor(hot[two], iota_wide[:], b3r(tab_lo[two].rearrange("p c r -> p (c r)"), P, CL * R), ALU.is_equal),
                    [("tab_lo", t)] + ([("sum_ps", t - 2)] if t >= 2 else []), ("hot", t))

            def ps_of(n, c):
                h = 2 * n + c // 4
                return bank[banks[h % len(banks)]][:, (c % 4) * SW:(c % 4 + 1) * SW], banks[h % len(banks)]

            def add_up(n):
                t = t0 + n
                for c in range(CL):
                    ps, b = ps_of(n, c)
                    needs = [("hot", t)] + (last_read[b] if c % 4 == 0 else [])
                    for i, (r, c0, w) in enumerate([(r, c0, w) for r in range(R) for c0, w in ((0, SW), (MID, A), (LOW, A))]):
                        pe(lambda e, c=c, ps=ps, i=i, r=r, c0=c0, w=w: e.matmul(ps[:, 0:w], hot[t % 2][:, :, c * R + r], tab[t % NTB][:, c, r, c0:c0 + w],
                                                                                start=i == 0, stop=i == 3 * R - 1),
                           needs, (("sum_ps", t) if c == CL - 1 else ("sum_ps4", t)) if (c % 4, i) == (3, 3 * R - 1) else None)
                    if c % 4 == 3:
                        last_read[b] = [("added", t, c)]

            def add_in(n):
                t = t0 + n
                at_of = [None] * CL
                for c in range(CL):
                    def emit(e, c=c):
                        if not regs:
                            regs.extend(e.alloc_register(f"column{i}") for i in range(CL))
                        if c == 0:
                            e.reg_load(regs, offs[0:1, t * CL:(t + 1) * CL])
                            at_of[:] = [e.snap(r, min_val=0, max_val=(NT - 1) * SW) for r in regs]
                        d = (sums, sums_odd)[c % 2][:, bass.ds(at_of[c], SW)]
                        return e.tensor_tensor(d, d, ps_of(n, c)[0], ALU.add)
                    before_it = [("added", t, c - 2)] if c >= 2 else ([("added", t - 1, CL - 2 + c)] if t else [])
                    dve(emit, [("sum_ps4", t) if c < 4 else ("sum_ps", t), ("sized", k)] + all_zeroed + before_it, ("added", t, c))

            return load, make_hot, add_up, add_in

        def sum_turns(k):
            load, make_hot, add_up, add_in = sum_steps(k)
            n_loads = loads[k]

            def before_products(n):
                if n == -1:
                    for m in range(min(NTB - 1, n_loads)):
                        load(m)
                if 0 <= n and n + NTB - 1 < n_loads:
                    load(n + NTB - 1)
                if n >= 1:
                    add_in(n - 1)
                if n + 1 < n_loads:
                    make_hot(n + 1)

            def products(n):
                if 0 <= n < n_loads:
                    add_up(n)
            return [(lambda n=n: before_products(n), lambda n=n: products(n)) for n in range(-1, n_loads + 1)]

        first_in_group, last_in_group = {}, {}
        for k in range(len(parts) - 1):
            g0, g1 = parts[k + 1]
            start = g0 + BEHIND + NP + 2
            turns = sum_turns(k)
            stop = g1 + BEHIND
            for i, (dve_half, pe_half) in enumerate(turns):
                g = start + i * (stop - start) // len(turns)
                first_in_group.setdefault(g, []).append(dve_half)
                last_in_group.setdefault(g, []).append(pe_half)

        for g in range(max(EG + BEHIND, max(at_group) + 1)):
            for step in first_in_group.get(g, []):
                step()
            for lag, stage in edge_stages:
                if 0 <= g - lag < EG:
                    stage(g - lag)
            if g % LG == 0 and g and g // LG + NA - 1 < NL:
                load_attr(g // LG + NA - 1)
            for step in at_group.get(g, []) + last_in_group.get(g, []):
                step()
        for b in (3, 4, 5):
            last_read[b] = [("fused_a", NG - 1), ("xt_a", NG - 1)]
        for dve_half, pe_half in sum_turns(len(parts) - 1):
            dve_half()
            pe_half()
        last = sum(loads) - 1
        summed = ("added", last, CL - 1)
        first_half_done = [(name, a) for a in range(max(0, NG - 2), NG) for name in ("x_ln", "fused_kept")]

        BX, BO, BH, BS, BG = (0, 1), (2, 3), (4, 5), 6, 7
        dve(lambda e: e.memset(minus_half, -0.5), [summed], "minus_half")
        dve(lambda e: e.memset(w5, 0.0), mark="w5_zero")
        dve(lambda e: e.memset(w5[:, :, 0, :, E_:E_ + 1], 1.0), ["w5_zero"], "w5_one")
        dve(lambda e: e.memset(fused[A:A + 1, :], 1.0), mark="fused_one")

        def half(i, t):
            return bank[i[t // 2]][:, (t % 2) * D:(t % 2 + 1) * D]

        def prev(name, g, back=1):
            return [(name, g - back)] if g >= back else []

        def load_xs(g):
            sp(lambda e: e.dma_start(xs[g % 2][:, 0:nt[g], :].rearrange("p t d -> p (t d)"), x_ln[g * P:(g + 1) * P, 0:nt[g] * D]),
               [summed] + first_half_done + prev("x1", g, 2), ("xs", g), s_xln_in[g % 2])
            sp(lambda e: e.dma_start(fused_in[g % 2][:, 0:nt[g] * P], fused_dram[g * A:(g + 1) * A, 0:nt[g] * P]),
               prev("pre", g, 2), ("fused_in", g), s_fused_in[g % 2])

        def light_mean(g):
            n = nt[g]
            cols = slice(g * TN * SW, (g * TN + n) * SW)
            s3 = time_sum[:, 0:n, :]
            dve(lambda e: e.tensor_tensor(s3.rearrange("p t c -> p (t c)"), sums[:, cols], sums_odd[:, cols], ALU.add), [summed] + prev("ntf", g), ("time_sum", g))
            dve(lambda e: e.tensor_scalar(cnt[:, 0:n], s3[:, :, A], 1.0, None, ALU.max), [("time_sum", g)], ("cnt", g))
            dve(lambda e: e.reciprocal(rcnt[:, 0:n], cnt[:, 0:n]), [("cnt", g)], ("rcnt", g))
            dve(lambda e: e.tensor_tensor(ntf[:, 0:n, :], s3[:, :, 0:A], b3d(rcnt[:, 0:n], n, A), ALU.mult),
                [("rcnt", g)] + prev("ntf_ps", g), ("ntf", g))

        def light_mean_t(g):
            n = nt[g]
            for t in range(n):
                pe(lambda e, t=t: e.transpose(bank[BS][0:A, t * P:(t + 1) * P], ntf[:, t, :], ident[:]),
                   [("ntf", g)] + prev("logits", g), ("ntf_ps", g) if t == n - 1 else None)
            act(lambda e: e.activation(ntf_t[:, 0:n * P], bank[BS][0:A, 0:n * P], ACT.Copy), [("ntf_ps", g)], ("ntf_t", g))

        def light_fuse(g):
            w = nt[g] * P
            pe(lambda e: e.matmul(bank[BS][0:A, 0:w], wf_time, ntf_t[:, 0:w], start=True, stop=True), [("ntf_t", g)], ("fuse_ps", g))
            dve(lambda e: e.tensor_tensor(pre[:, 0:w], bank[BS][0:A, 0:w], fused_in[g % 2][:, 0:w], ALU.add),
                [("fuse_ps", g), ("fused_in", g)] + prev("fused", g), ("pre", g))
            act(lambda e: e.activation(fused[0:A, 0:w], pre[:, 0:w], ACT.Relu), [("pre", g)], ("fused", g))

        def light_up(g):
            n = nt[g]
            xq = x1[g % 2]
            for t in range(n):
                pe(lambda e, t=t: e.matmul(half(BX, t), fused[:, t * P:(t + 1) * P], wu, start=True, stop=True),
                   [("fused", g), "fused_one"] + prev("yt", g), ("up", g) if t == n - 1 else None)
            for t in range(0, n, 2):
                m = min(2, n - t)
                dve(lambda e, t=t, m=m: e.tensor_tensor(xq[:, t:t + m, :].rearrange("p t d -> p (t d)"), xs[g % 2][:, t:t + m, :].rearrange("p t d -> p (t d)"),
                                                        bank[BX[t // 2]][:, 0:m * D], ALU.add),
                    [("up", g), ("xs", g)] + prev("o", g, 2), ("x1", g) if t + 2 >= n else ("x1a", g))
            for t in range(n):
                dve(lambda e, t=t: e.bn_stats(stat[:, t, :], xq[:, t, :]), [("x1", g)], ("stat", g, t))
            for t in range(n):
                dve(lambda e, t=t: e.bn_aggr(mv[:, t, :], stat[:, t, :]), [("stat", g, t)] + prev("xn", g), ("mv", g, t))
            dve(lambda e: e.tensor_scalar(var_eps[:, 0:n], mv[:, 0:n, 1], EPS, None, ALU.add), [("mv", g, n - 1)], ("var_eps", g))
            pool(lambda e: e.tensor_tensor(rs[:, 0:n], var_eps[:, 0:n], minus_half[:, 0:n], ALU.pow), [("var_eps", g), "minus_half"] + prev("xn", g), ("rs", g))
            for t in range(n):
                dve(lambda e, t=t: e.tensor_scalar(xn[:, t, :], xq[:, t, :], mv[:, t, 0:1], rs[:, t:t + 1], ALU.subtract, ALU.mult),
                    [("rs", g)] + prev("y_ps", g), ("xn", g) if t == n - 1 else None)

        def light_y_t(g):
            n = nt[g]
            for k in range(K):
                for t in range(n):
                    pe(lambda e, k=k, t=t: e.transpose(bank[BX[k]][:, t * P:(t + 1) * P], xn[:, t, k * P:(k + 1) * P], ident[:]),
                       [("xn", g)], ("y_ps", g) if (k, t) == (K - 1, n - 1) else None)
            for k in range(K):
                act(lambda e, k=k: e.activation(yt[:, k, 0:n * P], bank[BX[k]][:, 0:n * P], ACT.Copy), [("y_ps", g)], ("yt", g, k))
            steps.value_of[("yt", g)] = steps.value_of[("yt", g, K - 1)]

        def light_y_halves(g):
            w = nt[g] * P
            for k in range(K):
                dve(lambda e, k=k: e.tensor_scalar(yt_top[:, k, 0:w].bitcast(i32), yt[:, k, 0:w].bitcast(i32), HIGH_BITS, None, ALU.bitwise_and),
                    [("yt", g, k)] + prev("yt_high1", g), ("yt_top", g, k))
                act(lambda e, k=k: e.activation(yt_halves[0][:, k, 0:w], yt_top[:, k, 0:w], ACT.Copy), [("yt_top", g, k)] + prev("e1_3", g), (f"yt_high{k}", g))
                dve(lambda e, k=k: e.tensor_tensor(yt_halves[1][:, k, 0:w], yt[:, k, 0:w], yt_top[:, k, 0:w], ALU.subtract),
                    [("yt_top", g, k)] + prev("e1_3", g), (f"yt_low{k}", g))

        def light_gate(g):
            n = nt[g]
            gp = bank[BS][:, 0:n * E_]
            for t in range(n):
                at = gp[:, t * E_:(t + 1) * E_]
                for k in range(K):
                    pe(lambda e, k=k, t=t, at=at: e.matmul(at, yt[:, k, t * P:(t + 1) * P], wg[:, k, :], start=k == 0, stop=k == K - 1),
                       [("yt", g), ("pre", g)], ("gate_ps", g) if (t, k) == (n - 1, K - 1) else None)
            g3 = gp.rearrange("p (t c) -> p t c", c=E_)
            dve(lambda e: e.tensor_tensor(sc[:, 0:n, :], g3, b3r(bg, n, E_), ALU.add), [("gate_ps", g)], ("logits", g))
            dve(lambda e: e.tensor_reduce(gm[:, 0:n], sc[:, 0:n, :], AX.X, ALU.max), [("logits", g)], ("gm", g))
            dve(lambda e: e.tensor_tensor(lg[:, 0:n, :], sc[:, 0:n, :], b3d(gm[:, 0:n], n, E_), ALU.subtract), [("gm", g)], ("lg", g))
            act(lambda e: e.activation(ge[:, 0:n, :], lg[:, 0:n, :], ACT.Exp), [("lg", g)], ("ge", g))

        def links(g, first, name):
            last = [first]

            def link(emit):
                mark = (name, g, len(last))
                dve(emit, [last[0]], mark)
                last.append(mark)
                last[0] = mark
            return last, link

        def light_top2(g):
            n = nt[g]
            last, link = links(g, ("ge", g), "top")
            v = lambda a: a[:, 0:n, :]
            c = lambda a: b3d(a[:, 0:n], n, E_)
            link(lambda e: e.tensor_reduce(m1[:, 0:n], v(ge), AX.X, ALU.add))
            link(lambda e: e.reciprocal(m2[:, 0:n], m1[:, 0:n]))
            link(lambda e: e.tensor_tensor(v(ge), v(ge), c(m2), ALU.mult))

            def pick(m, sel):
                link(lambda e: e.tensor_reduce(m[:, 0:n], v(ge), AX.X, ALU.max))
                link(lambda e: e.tensor_tensor(v(sc), v(ge), c(m), ALU.is_equal))
                link(lambda e: e.tensor_tensor(v(sc), v(sc), b3r(first_rank[:], n, E_), ALU.mult))
                link(lambda e: e.tensor_reduce(mt[:, 0:n], v(sc), AX.X, ALU.max))
                link(lambda e: e.tensor_tensor(v(sel), v(sc), c(mt), ALU.is_equal))
            pick(m1, sel1)
            link(lambda e: e.scalar_tensor_tensor(v(ge), v(sel1), -2.0, v(ge), ALU.mult, ALU.add))
            pick(m2, sel2)
            link(lambda e: e.tensor_tensor(mt[:, 0:n], m2[:, 0:n], m1[:, 0:n], ALU.subtract))
            steps.value_of[("gap", g)] = steps.value_of[last[0]]

        def light_weights(g):
            n = nt[g]
            act(lambda e: e.activation(wb[:, 0:n], mt[:, 0:n], ACT.Exp), [("gap", g)], ("exp_gap", g))
            last, link = links(g, ("exp_gap", g), "weigh")
            v = lambda a: a[:, 0:n, :]
            c = lambda a: b3d(a[:, 0:n], n, E_)
            link(lambda e: e.tensor_scalar(mt[:, 0:n], wb[:, 0:n], 1.0, None, ALU.add))
            link(lambda e: e.reciprocal(wa[:, 0:n], mt[:, 0:n]))
            link(lambda e: e.tensor_tensor(wb[:, 0:n], wb[:, 0:n], wa[:, 0:n], ALU.mult))
            link(lambda e: e.tensor_tensor(v(sel1), v(sel1), c(wa), ALU.mult))
            link(lambda e: e.tensor_tensor(v(sel2), v(sel2), c(wb), ALU.mult))
            link(lambda e: e.tensor_tensor(v(w4), v(sel1), v(sel2), ALU.add))
            link(lambda e: e.tensor_copy(v(w4_high), v(w4)))
            link(lambda e: e.tensor_tensor(v(w4_rest), v(w4), v(w4_high), ALU.subtract))
            link(lambda e: e.tensor_copy(v(w4_mid), v(w4_rest)))

            for t in range(n):
                three = lambda a, t=t: a[:, t:t + 1, :].to_broadcast([P, 3, E_])
                dve(lambda e, t=t, three=three: e.tensor_copy(w5[:, t, 0, :, 0:E_], three(w4_high)), [last[0]] + prev("w5_ps", g))
                dve(lambda e, t=t, three=three: e.tensor_copy(w5[:, t, 1, :, 0:E_], three(w4_mid)))
                dve(lambda e, t=t, three=three: e.tensor_tensor(w5[:, t, 2, :, 0:E_], three(w4_rest), three(w4_mid), ALU.subtract),
                    (), ("w5", g) if t == n - 1 else None)

        uses = [0]

        def hidden(g, name, out_sb, needs, parts, bias):
            w = nt[g] * P
            u = uses[0]
            uses[0] += 1
            b = bank[BH[u % 2]]
            for i, (po, pn, lhs, rhs, first, final) in enumerate(parts):
                pe(lambda e, po=po, pn=pn, lhs=lhs, rhs=rhs, first=first, final=final: e.matmul(b[po:po + pn, 0:w], lhs, rhs, start=first, stop=final),
                   needs + ([("hid", u - 2)] if u >= 2 else []), ("hid_ps", u) if i == len(parts) - 1 else None)
            act(lambda e: e.activation(out_sb, b[:, 0:w], ACT.Relu, bias=bias), [("hid_ps", u)], ("hid", u))
            steps.value_of[(name, g)] = steps.value_of[("hid", u)]

        def from_halves(g, weight):
            halves_of = [(f"yt_{half}{k}", g) for k in range(K) for half in ("high", "low")]
            terms = [(k, a, b) for k in range(K) for a, b in ((0, 0), (1, 0), (0, 1))]
            return halves_of, [(0, P, weight(a, k), yt_halves[b][:, k, 0:nt[g] * P], i == 0, i == len(terms) - 1) for i, (k, a, b) in enumerate(terms)]

        def shared1(g, m):
            hidden(g, f"h1_{m}", h1[:, m, 0:nt[g] * P], *from_halves(g, lambda a, k: w1[a][:, k, m * P:(m + 1) * P]), b_1[:, m:m + 1])

        def shared2(g):
            w = nt[g] * P
            hidden(g, "h2", h2[:, 0:w], [("h1_0", g), ("h1_1", g)], [(0, P, w2[:, k, :], h1[:, k, 0:w], k == 0, k == K - 1) for k in range(K)], b_2)

        def expert1(g, x_):
            hidden(g, f"e1_{x_}", e1[:, x_, 0:nt[g] * P], *from_halves(g, lambda a, k: we1[a][:, x_, k, :]), b_e1[:, x_:x_ + 1])

        def expert2(g, q):
            w = nt[g] * P
            hidden(g, f"e2_{q}", e2r[:, q, 0:w], [(f"e1_{2 * q}", g), (f"e1_{2 * q + 1}", g)],
                   [(i * H2, H2, we2[:, 2 * q + i, :], e1[:, 2 * q + i, 0:w], True, True) for i in range(2)],
                   b_e2[:, q:q + 1])

        def weights_t(g):
            n = nt[g]
            for t in range(n):
                pe(lambda e, t=t: e.transpose(bank[BG][0:S, t * P:(t + 1) * P], w5[:, t, :, :, :].rearrange("p i j e -> p (i j e)"), ident[:]),
                   [("w5", g)], ("w5_ps", g) if t == n - 1 else None)
            act(lambda e: e.activation(w5_t[:, 0:n * P], bank[BG][0:S, 0:n * P], ACT.Copy), [("w5_ps", g)], ("w5_t", g))

        def spread(g, q):
            n = nt[g]
            pe(lambda e: e.matmul(bank[BG][:, 0:n * P], spread_bf[:, q, :], w5_t[:, 0:n * P], start=True, stop=True),
               [("w5_t", g) if q == 0 else ("mul0", g)], (f"spread{q}", g))
            dve(lambda e: e.tensor_tensor(e2[:, q, 0:n * P], e2r[:, q, 0:n * P], bank[BG][:, 0:n * P], ALU.mult),
                [(f"spread{q}", g), (f"e2_{q}", g)] + prev("out_ps", g), (f"mul{q}", g))

        def final(g, part):
            n = nt[g]
            if part == 0:
                terms = [(h2, w3, ("h2", g)), (w5_t, b3_bf[:], ("w5_t", g)), (e2[:, 0, :], we3[:, 0, :], ("mul0", g))]
            else:
                terms = [(e2[:, 1, :], we3[:, 1, :], ("mul1", g))]
            for i, (lhs, rhs, need) in enumerate(terms):
                for t in range(n):
                    pe(lambda e, t=t, i=i, lhs=lhs, rhs=rhs: e.matmul(half(BO, t), lhs[:, t * P:(t + 1) * P], rhs, start=part == 0 and i == 0 and t % 2 == 0,
                                                                      stop=part == 1, skip_group_check=True),
                       [need] + (prev("o", g) if part == 0 else []), ("out_ps", g) if (part, t) == (1, n - 1) else None)

        def finish(g):
            n = nt[g]
            for t in range(0, n, 2):
                m = min(2, n - t)
                dve(lambda e, t=t, m=m: e.tensor_tensor(o[g % 2][:, t:t + m, :].rearrange("p t d -> p (t d)"), x1[g % 2][:, t:t + m, :].rearrange("p t d -> p (t d)"),
                                                        bank[BO[t // 2]][:, 0:m * D], ALU.add),
                    [("out_ps", g)] + prev("stored", g, 2), ("o", g) if t + 2 >= n else None)
            full = sum(r == P for r in rows[g])
            r0 = g * TN * P
            if full:
                sp(lambda e: e.dma_start(out[r0:r0 + full * P, :].rearrange("(t p) d -> p t d", p=P), o[g % 2][:, 0:full, :]),
                   [("o", g)], ("stored_full", g), s_out[g % 2])
            if full < n:
                sp(lambda e: e.dma_start(out[r0 + full * P:N, :], o[g % 2][0:rows[g][-1], full, :]), [("o", g)], ("stored_part", g), s_out[g % 2])
            steps.value_of[("stored", g)] = steps.value_of[("stored_part" if full < n else "stored_full", g)]

        load_xs(0)
        light_mean(0)
        for i in range(NG + 1):
            heavy, light = i - 1 if i else None, i if i < NG else None
            after = i + 1 if i + 1 < NG else None
            both = [
                (heavy, lambda g: shared1(g, 0)), (heavy, lambda g: shared1(g, 1)), (light, light_mean_t),
                (heavy, lambda g: expert1(g, 0)), (light, light_fuse), (heavy, light_weights), (heavy, lambda g: expert1(g, 1)),
                (heavy, shared2), (light, light_up), (heavy, lambda g: expert1(g, 2)),
                (heavy, weights_t), (heavy, lambda g: expert2(g, 0)), (heavy, lambda g: spread(g, 0)), (heavy, lambda g: expert1(g, 3)),
                (heavy, lambda g: final(g, 0)), (light, light_y_t), (heavy, lambda g: expert2(g, 1)),
                (heavy, lambda g: spread(g, 1)), (light, light_y_halves), (after, light_mean), (light, light_gate), (heavy, lambda g: final(g, 1)),
                (light, light_top2), (heavy, finish),
            ]
            if i + 1 < NG:
                load_xs(i + 1)
            for g, step in both:
                if g is not None:
                    step(g)

        def wait_outputs(e):
            for g in range(max(0, NG - 2), NG):
                at, value = steps.value_of[("stored", g)]
                e.wait_ge(at, value)

        with nc.Block() as block:
            @block.sync
            def _(e):
                steps.emit("sp", e)
                wait_outputs(e)

            @block.tensor
            def _(e):
                steps.emit("pe", e)

            @block.vector
            def _(e):
                steps.emit("dve", e)

            @block.scalar
            def _(e):
                steps.emit("act", e)

            @block.gpsimd
            def _(e):
                steps.emit("pool", e)


def kernel(**inputs):
    import concourse.bacc as bacc
    from concourse.bass_utils import run_bass_kernel_spmd

    a = {k: np.asarray(v) for k, v in inputs.items()}
    n, d = a["x"].shape
    edges, ed = a["edge_attr_32"].shape
    node_tiles = -(-n // P)
    tg = 5
    tiles = -(-edges // (P * tg)) * tg
    assert n < node_tiles * P
    src = np.full((tiles * P,), node_tiles * P - 1, np.int32)
    src[:edges] = a["src"]
    attr = np.zeros((ed, tiles * P), np.float32)
    attr[:, :edges] = a["edge_attr_32"].T
    g, f = "L0_gnn_", "L0_ffn_"

    def by_partition(w):
        return w.reshape(-1, P, w.shape[-1]).transpose(1, 0, 2)

    ew1, ew2, ew3 = a[f + "eW1"], a[f + "eW2"], a[f + "eW3"]
    e, _, h1 = ew1.shape
    h2 = ew2.shape[2]
    row = np.arange(9 * (e + 1))
    part_j, expert = row // (e + 1) % 3, row % (e + 1)
    b3_part = part_j[:, None] == np.arange(3)
    spread = (part_j == 0)[:, None, None] & (expert[:, None, None] == (np.arange(e // 2)[:, None] * 2 + np.arange(P) // h2))
    parts = {
        "wd": by_partition(a[g + "W_down"].T), "wt": np.vstack([a[g + "W_time"].T, a[g + "b_time"][None]]),
        "wf_node": a[g + "W_fusion"].T[:len(a[g + "b_down"])], "wf_time": a[g + "W_fusion"].T[len(a[g + "b_down"]):],
        "wu": np.vstack([a[g + "W_up"].T, a[g + "b_up"][None]]),
        "w1": by_partition(a[f + "sW1"]), "w2": by_partition(a[f + "sW2"]), "w3": a[f + "sW3"],
        "we1": ew1.reshape(e, -1, P, h1).transpose(2, 0, 1, 3), "we2": ew2.transpose(1, 0, 2),
        "we3": ew3.reshape(e // 2, 2 * h2, -1).transpose(1, 0, 2), "b3": np.tile(np.vstack([a[f + "eb3"], a[f + "sb3"][None]]), (9, 1)), "b3_part": b3_part, "spread": spread,
        "wg": by_partition(a[f + "gW"]), "bg": np.broadcast_to(a[f + "gb"], (P, e)),
        "b_d": a[g + "b_down"][:, None], "b_f": a[g + "b_fusion"][:, None],
        "b_1": a[f + "sb1"].reshape(-1, P).T, "b_2": a[f + "sb2"][:, None],
        "b_e1": a[f + "eb1"].T, "b_e2": a[f + "eb2"].reshape(e // 2, -1).T,
    }
    dims = (d, len(a[g + "b_down"]), ed, a[f + "sW1"].shape[1], a[f + "sW2"].shape[1], e, h1, h2, ew3.shape[2])
    columns = weight_columns(*dims)
    weights = np.zeros((P, sum(int(np.prod(shape)) for _, shape in columns.values())), np.float32)
    at = 0
    for name, (used, shape) in columns.items():
        free = int(np.prod(shape))
        weights[:used, at:at + free] = parts[name].reshape(used, free)
        at += free
    given = [("x", a["x"]), ("src_t", src.reshape(tiles, P).T), ("attr_t", attr), ("weights", weights)]

    nc = bacc.Bacc("TRN2", target_bir_lowering=False, num_devices=1)
    arrays, args = {}, []
    for name, v in given:
        v = np.ascontiguousarray(v)
        arrays[f"in_{name}"] = v
        args.append(nc.dram_tensor(f"in_{name}", v.shape, mybir.dt.from_np(v.dtype), kind="ExternalInput").ap())
    args.append(nc.dram_tensor("out_rows", (n, d), mybir.dt.float32, kind="ExternalOutput").ap())
    gnn_ffn(nc, *args[:-1], dims, args[-1])
    return run_bass_kernel_spmd(nc, [arrays], core_ids=[0]).results[0]["out_rows"]
```
